# Optimizing a Trainium2 kernel written in Bass

```python
import numpy as np
import jax
import jax.numpy as jnp

def _softmax(x, axis=-1):
    return jax.nn.softmax(x, axis=axis)

def _gelu(x):
    return jax.nn.gelu(x, approximate=True)

def _silu(x):
    return jax.nn.silu(x)

def _sigmoid(x):
    return jax.nn.sigmoid(x)

def _layernorm(x, axis=-1, eps=1e-05):
    m = jnp.mean(x, axis=axis, keepdims=True)
    v = jnp.var(x, axis=axis, keepdims=True)
    return (x - m) / jnp.sqrt(v + eps)

def _scatter_add(tgt, idx, src, axis=0):
    return tgt.at[idx].add(src)

def _segment_sum(src, seg, n):
    return jax.ops.segment_sum(src, seg, n)
kernel_name = 'mk_gps_d1_gnn_r64_0b5dbc'

def setup_inputs(seed: int=0):
    np.random.seed(seed)
    _w = jnp.asarray

    def _rec_inputs():
        import jax
        import jax.numpy as jnp
        _gk = jax.random.key(seed)
        x = -0.0001538 + 1 * jax.random.normal(jax.random.fold_in(_gk, 1), (128, 768), jnp.float32)
        src = jax.random.randint(jax.random.fold_in(_gk, 2), (4096,), 0, 128, jnp.int32)
        dst = jnp.minimum((128 * jax.random.uniform(jax.random.fold_in(_gk, 3), (4096,)) ** 2.0).astype(jnp.int32), 8191)
        _o = jnp.argsort(dst, stable=True)
        src = src[_o]
        dst = dst[_o]
        return (x, src, dst)
    x, src, dst = _rec_inputs()

    def _L0_gnn_setup():
        import jax, jax.numpy as jnp
        import numpy as np
        NEG_SLOPE = 0.2
        EPS = 1e-16
        N_NODES = 128
        N_EDGES = 1024
        D_IN = 768
        D_HID = 768
        H1 = 8
        H2 = 1

        def gat_layer(x, W, a_s, a_d, b, edge_index, concat):
            n = x.shape[0]
            H, C = a_s.shape
            h = (x @ W).reshape(n, H, C)
            src, dst = (edge_index[0], edge_index[1])
            alpha_s = jnp.einsum('nhc,hc->nh', h, a_s)
            alpha_d = jnp.einsum('nhc,hc->nh', h, a_d)
            e = jax.nn.leaky_relu(alpha_s[src] + alpha_d[dst], NEG_SLOPE)
            m = jax.ops.segment_max(e, dst, num_segments=n)
            e = jnp.exp(e - m[dst])
            denom = jax.ops.segment_sum(e, dst, num_segments=n)
            alpha = e / (denom[dst] + EPS)
            msg = h[src] * alpha[:, :, None]
            out = jax.ops.segment_sum(msg, dst, num_segments=n)
            out = out.reshape(n, H * C) if concat else out.mean(axis=1)
            return out + b
        key = jax.random.key(seed)
        ks = jax.random.split(key, 10)
        x = jax.random.normal(ks[0], (N_NODES, D_IN), dtype=jnp.float32)
        edge_list = jax.random.randint(ks[1], (2, N_EDGES), 0, N_NODES, dtype=jnp.int32)
        s = 0.05
        W1 = jax.random.normal(ks[2], (D_IN, H1 * D_HID), dtype=jnp.float32) * s
        a_src1 = jax.random.normal(ks[3], (H1, D_HID), dtype=jnp.float32) * s
        a_dst1 = jax.random.normal(ks[4], (H1, D_HID), dtype=jnp.float32) * s
        b1 = jnp.zeros((H1 * D_HID,), dtype=jnp.float32)
        W2 = jax.random.normal(ks[5], (H1 * D_HID, H2 * D_HID), dtype=jnp.float32) * s
        a_src2 = jax.random.normal(ks[6], (H2, D_HID), dtype=jnp.float32) * s
        a_dst2 = jax.random.normal(ks[7], (H2, D_HID), dtype=jnp.float32) * s
        b2 = jnp.zeros((H2 * D_HID,), dtype=jnp.float32)
        return {'x': x, 'W1': W1, 'a_src1': a_src1, 'a_dst1': a_dst1, 'b1': b1, 'W2': W2, 'a_src2': a_src2, 'a_dst2': a_dst2, 'b2': b2, 'edge_list': edge_list}
    _L0_gnn_all = _L0_gnn_setup()
    _L0_gnn_in = {k: v for k, v in _L0_gnn_all.items() if k in ('W1', 'a_src1', 'a_dst1', 'b1', 'W2', 'a_src2', 'a_dst2', 'b2')}
    del _L0_gnn_all

    def _L0_mix_setup():
        import jax, jax.numpy as jnp
        import numpy as np
        import math
        EPS = 0.001

        def _relu_features(t, proj_mat):
            ratio = 1.0 / math.sqrt(float(proj_mat.shape[0]))
            z = ratio * jnp.einsum('blhd,md->blhm', t, proj_mat)
            return jax.nn.relu(z) + EPS
        key = jax.random.key(seed)
        ks = jax.random.split(key, 6)
        B, L, DIM = (8, 64, 768)
        H, D, M = (12, 64, 256)
        x = jax.random.normal(ks[0], (B, L, DIM), dtype=jnp.float32)
        qkv_w = jax.random.normal(ks[1], (3 * DIM, DIM), dtype=jnp.float32) * DIM ** (-0.5)
        qkv_b = jnp.zeros((3 * DIM,), dtype=jnp.float32)
        proj_w = jax.random.normal(ks[2], (DIM, DIM), dtype=jnp.float32) * DIM ** (-0.5)
        proj_b = jnp.zeros((DIM,), dtype=jnp.float32)
        blocks = []
        for i in range(M // D):
            g = jax.random.normal(ks[3 + 0] if False else jax.random.fold_in(ks[3], i), (D, D), dtype=jnp.float32)
            q, _ = jnp.linalg.qr(g)
            blocks.append(q.T)
        pm = jnp.concatenate(blocks, axis=0)
        mult = jnp.linalg.norm(jax.random.normal(ks[4], (M, D), dtype=jnp.float32), axis=1)
        proj_mat = mult[:, None] * pm
        return {'x': x, 'qkv_w': qkv_w, 'qkv_b': qkv_b, 'proj_w': proj_w, 'proj_b': proj_b, 'proj_mat': proj_mat}
    _L0_mix_all = _L0_mix_setup()
    _L0_mix_in = {k: v for k, v in _L0_mix_all.items() if k in ('qkv_w', 'qkv_b', 'proj_w', 'proj_b', 'proj_mat')}
    del _L0_mix_all

    def _L0_ffn_setup():
        import jax, jax.numpy as jnp
        import numpy as np
        B, S, D_IN, D_HID, D_OUT = (32, 512, 768, 48, 768)
        key = jax.random.key(seed)
        k1, k2, k3, k4 = jax.random.split(key, 4)
        init_k = float(np.sqrt(1.0 / D_IN))
        init_k2 = float(np.sqrt(1.0 / D_HID))
        x = jax.random.normal(k1, (B, S, D_IN), dtype=jnp.float32)
        in_weight = jax.random.uniform(k2, (D_HID, D_IN), dtype=jnp.float32, minval=-init_k, maxval=init_k)
        in_bias = jax.random.uniform(k3, (D_HID,), dtype=jnp.float32, minval=-init_k, maxval=init_k)
        out_weight = jax.random.uniform(k4, (D_HID, D_OUT), dtype=jnp.float32, minval=-init_k2, maxval=init_k2)
        return {'x': x, 'in_weight': in_weight, 'in_bias': in_bias, 'out_weight': out_weight}
    _L0_ffn_all = _L0_ffn_setup()
    _L0_ffn_in = {k: v for k, v in _L0_ffn_all.items() if k in ('in_weight', 'in_bias', 'out_weight')}
    del _L0_ffn_all
    return {'x': x, 'src': src, 'dst': dst, 'L0_gnn_W1': _L0_gnn_in['W1'], 'L0_gnn_a_src1': _L0_gnn_in['a_src1'], 'L0_gnn_a_dst1': _L0_gnn_in['a_dst1'], 'L0_gnn_b1': _L0_gnn_in['b1'], 'L0_gnn_W2': _L0_gnn_in['W2'], 'L0_gnn_a_src2': _L0_gnn_in['a_src2'], 'L0_gnn_a_dst2': _L0_gnn_in['a_dst2'], 'L0_gnn_b2': _L0_gnn_in['b2'], 'L0_mix_qkv_w': _L0_mix_in['qkv_w'], 'L0_mix_qkv_b': _L0_mix_in['qkv_b'], 'L0_mix_proj_w': _L0_mix_in['proj_w'], 'L0_mix_proj_b': _L0_mix_in['proj_b'], 'L0_mix_proj_mat': _L0_mix_in['proj_mat'], 'L0_ffn_in_weight': _L0_ffn_in['in_weight'], 'L0_ffn_in_bias': _L0_ffn_in['in_bias'], 'L0_ffn_out_weight': _L0_ffn_in['out_weight']}

def reference(x, src, dst, L0_gnn_W1, L0_gnn_a_src1, L0_gnn_a_dst1, L0_gnn_b1, L0_gnn_W2, L0_gnn_a_src2, L0_gnn_a_dst2, L0_gnn_b2, L0_mix_qkv_w, L0_mix_qkv_b, L0_mix_proj_w, L0_mix_proj_b, L0_mix_proj_mat, L0_ffn_in_weight, L0_ffn_in_bias, L0_ffn_out_weight):
    import jax
    import jax.numpy as jnp

    def _L0_gnn_ref(x, W1, a_src1, a_dst1, b1, W2, a_src2, a_dst2, b2, edge_list):
        import jax, jax.numpy as jnp
        import numpy as np
        NEG_SLOPE = 0.2
        EPS = 1e-16
        N_NODES = 128
        N_EDGES = 1024
        D_IN = 768
        D_HID = 768
        H1 = 8
        H2 = 1

        def gat_layer(x, W, a_s, a_d, b, edge_index, concat):
            n = x.shape[0]
            H, C = a_s.shape
            h = (x @ W).reshape(n, H, C)
            src, dst = (edge_index[0], edge_index[1])
            alpha_s = jnp.einsum('nhc,hc->nh', h, a_s)
            alpha_d = jnp.einsum('nhc,hc->nh', h, a_d)
            e = jax.nn.leaky_relu(alpha_s[src] + alpha_d[dst], NEG_SLOPE)
            m = jax.ops.segment_max(e, dst, num_segments=n)
            e = jnp.exp(e - m[dst])
            denom = jax.ops.segment_sum(e, dst, num_segments=n)
            alpha = e / (denom[dst] + EPS)
            msg = h[src] * alpha[:, :, None]
            out = jax.ops.segment_sum(msg, dst, num_segments=n)
            out = out.reshape(n, H * C) if concat else out.mean(axis=1)
            return out + b
        h = gat_layer(x, W1, a_src1, a_dst1, b1, edge_list, concat=True)
        h = jax.nn.elu(h)
        out = gat_layer(h, W2, a_src2, a_dst2, b2, edge_list, concat=True)
        return out

    def _L0_mix_ref(x, qkv_w, qkv_b, proj_w, proj_b, proj_mat):
        import jax, jax.numpy as jnp
        import numpy as np
        import math
        EPS = 0.001

        def _relu_features(t, proj_mat):
            ratio = 1.0 / math.sqrt(float(proj_mat.shape[0]))
            z = ratio * jnp.einsum('blhd,md->blhm', t, proj_mat)
            return jax.nn.relu(z) + EPS
        B, L, DIM = x.shape
        H = 12
        D = DIM // H
        qkv = x @ qkv_w.T + qkv_b
        qkv = qkv.reshape(B, L, 3, H, D)
        q, k, v = (qkv[:, :, 0], qkv[:, :, 1], qkv[:, :, 2])
        q_p = _relu_features(q, proj_mat)
        k_p = _relu_features(k, proj_mat)
        kv = jnp.einsum('blhm,blhd->bhmd', k_p, v)
        k_sum = k_p.sum(axis=1)
        num = jnp.einsum('blhm,bhmd->blhd', q_p, kv)
        den = jnp.einsum('blhm,bhm->blh', q_p, k_sum)
        out = num / den[..., None]
        out = out.reshape(B, L, DIM)
        return out @ proj_w.T + proj_b

    def _L0_ffn_ref(x, in_weight, in_bias, out_weight):
        import jax, jax.numpy as jnp
        import numpy as np
        B, S, D_IN, D_HID, D_OUT = (32, 512, 768, 48, 768)
        lead = x.shape[:-1]
        xt = x.reshape(-1, in_weight.shape[1])
        h = jax.nn.gelu(jnp.einsum('td,hd->th', xt, in_weight) + in_bias, approximate=False)
        out = jnp.einsum('th,ho->to', h, out_weight)
        return out.reshape(*lead, out_weight.shape[1])
    edge_index = jnp.stack([src, dst])
    xn = _layernorm(x, axis=-1)
    x = x + _L0_gnn_ref(xn, L0_gnn_W1, L0_gnn_a_src1, L0_gnn_a_dst1, L0_gnn_b1, L0_gnn_W2, L0_gnn_a_src2, L0_gnn_a_dst2, L0_gnn_b2, edge_index) + _L0_mix_ref(xn[None], L0_mix_qkv_w, L0_mix_qkv_b, L0_mix_proj_w, L0_mix_proj_b, L0_mix_proj_mat)[0]
    x = x + _L0_ffn_ref(_layernorm(x, axis=-1)[None], L0_ffn_in_weight, L0_ffn_in_bias, L0_ffn_out_weight)[0]
    return x

_drawn_inputs = setup_inputs


def setup_inputs(seed=0):
    import zlib

    import numpy as np

    out = dict(_drawn_inputs(seed))
    spreads = {'L0_gnn_b1': (0.0, 0.1),
     'L0_gnn_b2': (0.0, 0.1),
     'L0_mix_qkv_b': (0.0, 0.1),
     'L0_mix_proj_b': (0.0, 0.1)}
    factors = {'L0_mix_proj_mat': 8.0, 'L0_ffn_in_bias': 8.0}
    for name, (base, spread) in spreads.items():
        noise = np.random.default_rng([zlib.crc32(name.encode()), seed]).standard_normal(out[name].shape)
        drawn = base * np.exp(spread * noise) if base else spread * noise
        out[name] = jnp.asarray(drawn.astype(out[name].dtype))
    for name, factor in factors.items():
        out[name] = (out[name] * factor).astype(out[name].dtype)
    return out
```

```python
from contextlib import ExitStack

import concourse.bass as bass
from concourse import mybir

ALU = mybir.AluOpType
ACT = mybir.ActivationFunctionType
F32 = mybir.dt.float32
F32R = mybir.dt.float32r
BF16 = mybir.dt.bfloat16
I32 = mybir.dt.int32

P = 128
D = 768
HEADS = 8
TB = D // P
HALF = D // 2
EDGES = 4096
EC = EDGES // P
MH, MD = 12, 64
MF = 256
PAIR = 2 * MD
HID = 48
LN_EPS = 1e-5
FEATURE_EPS = 1e-3
DENOM_EPS = 1e-16
SLOPE = 0.2
FAR = 1e30

STEPS_PER_LOAD = 3
GROUPS = ([("head", h, TB) for h in range(HEADS)] + [("q", 0, TB), ("k", 1, TB), ("v", 2, TB)]
          + [("layer2", 0, HEADS * TB), ("out", 0, TB)])
STEPS = [(g, j) for g, (_, _, n) in enumerate(GROUPS) for j in range(n)]
G_Q, G_K, G_V, G_L2, G_OUT = range(HEADS, HEADS + 5)
FIRST = [sum(n for _, _, n in GROUPS[:g]) for g in range(len(GROUPS))]
LAST = [sum(n for _, _, n in GROUPS[:g + 1]) - 1 for g in range(len(GROUPS))]
LOADS = len(STEPS) // STEPS_PER_LOAD
RAW = 5
PARTS = 6
LEAD = 4

SPLIT = [not (g < HEADS and (s < 3 or s % 4 == 0)) for s, (g, _) in enumerate(STEPS)]
SPLITS_BY = [sum(SPLIT[:s + 1]) for s in range(len(STEPS))]
NTH_SPLIT = [s for s in range(len(STEPS)) if SPLIT[s]]

CHAINS = [(c, c) for c in range(HEADS)] + [(HEADS, G_L2)]
AT_TURN, AT_ALPHA, AT_ROW, AT_ATT, AT_AGG, AT_ELU, AT_PARTS = 1, 3, 4, 7, 9, 10, 11
TAIL_ALPHA, TAIL_ROW, TAIL_ATT = 2, 3, 5
PAIR_FIRST = FIRST[G_L2] + 2
PAIR_EVERY = 7
AT_AO = PAIR_FIRST + PAIR_EVERY * TB


def build_gps_layer(nc, x, src, dst, w1, w2, qkv, proj, a1, a2, b1, rows, pm, w_in, b_in, w_out, out):
    ctx = ExitStack()
    with ctx:
        def sb(name, shape, dt=F32):
            return ctx.enter_context(nc.sbuf_tensor(name, shape, dt))

        def ps(name, shape):
            return ctx.enter_context(nc.psum_tensor(name, shape, F32))

        def sem(name):
            return ctx.enter_context(nc.semaphore(name))

        raw = sb("raw", [P, RAW, STEPS_PER_LOAD, D])
        w_hi = sb("w_hi", [P, PARTS, D], F32R)
        w_lo = sb("w_lo", [P, PARTS, D], F32R)
        hid_hi = sb("hid_hi", [P, HEADS * TB, P], F32R)
        hid_lo = sb("hid_lo", [P, HEADS * TB, P], F32R)
        xT = sb("xT", [P, TB, P])
        xT_hi = sb("xT_hi", [P, TB, P], F32R)
        xT_lo = sb("xT_lo", [P, TB, P], F32R)
        x_sb = sb("x_sb", [P, D])
        h_hi = sb("h_hi", [P, 2, D], F32R)
        h_lo = sb("h_lo", [P, 2, D], F32R)
        hT = sb("hT", [P, TB, P])
        yt = sb("yt", [P, D])
        et = sb("et", [P, D])
        hf = sb("hf", [P, D])
        scratch = sb("scratch", [P, 4176])
        qk = sb("qk", [P, D])
        count = sb("count", [P, P])
        absent = sb("absent", [P, P])
        score = sb("score", [P, P])
        leaky = sb("leaky", [P, P])
        masked = sb("masked", [P, P])
        expo = sb("expo", [P, P])
        weight = sb("weight", [P, P])
        att = sb("att", [P, P])
        diag = sb("diag", [P, P])
        ident = sb("ident", [P, P])
        ident_r = sb("ident_r", [P, P], F32R)
        ones = sb("ones", [P, P])
        column = sb("column", [P, P])
        attT_hi = sb("attT_hi", [P, P], F32R)
        attT_lo = sb("attT_lo", [P, P], F32R)
        row_sb = sb("row_sb", [5, D])
        pick = sb("pick", [5, 4, P])
        pm_sb = sb("pm_sb", [P, MF])
        a1_sb = sb("a1_sb", [P, HEADS, TB, 2])
        a2_sb = sb("a2_sb", [P, TB, 2])
        b1_sb = sb("b1_sb", [P, HEADS, TB])
        w_in_sb = sb("w_in_sb", [P, TB, HID])
        b_in_sb = sb("b_in_sb", [HID, 1])
        w_out_sb = sb("w_out_sb", [HID, D])
        f_hid = sb("f_hid", [HID, P])
        ends = sb("ends", [P, 2, EC], I32)
        endf = sb("endf", [P, 2, EC])
        kv = sb("kv", [P, 4, MD + 1])
        alpha = sb("alpha", [P, 2])
        stats = sb("stats", [P, 2, 6])
        mv = sb("mv", [P, 2])
        vpe = sb("vpe", [P, 1])
        rstd = sb("rstd", [P, 1])
        minus_half = sb("minus_half", [P, 1])
        top = sb("top", [P, 1])
        ntop = sb("ntop", [P, 1])
        den = sb("den", [P, 1])
        dene = sb("dene", [P, 1])
        rden = sb("rden", [P, 1])
        mrec = sb("mrec", [P, 2])

        hot = scratch[:, 0:2 * EC * P // 2].bitcast(BF16).rearrange("p (a c n) -> p a c n", a=2, c=EC)
        qT = scratch[:, 0:D].rearrange("p (t n) -> p t n", t=TB)
        kT = scratch[:, D:2 * D].rearrange("p (t n) -> p t n", t=TB)
        v1 = scratch[:, 2 * D:2 * D + MH * (MD + 1)].rearrange("p (h d) -> p h d", h=MH)
        AO0 = 2 * D + MH * (MD + 1)
        ao = scratch[:, AO0:AO0 + D]
        feats = scratch[:, AO0 + D:AO0 + D + 1024].rearrange("p (a f) -> p a f", a=2)
        xn = hf

        acc = [ps(f"acc{i}", [P, 2, 512]) for i in range(2)]
        wk = ps("wk", [P, 2, 512])
        small = ps("small", [P, 512])
        plane = ps("plane", [P, 512])

        def blocks(bank):
            return bank[:, :, 0:HALF]

        def block(bank, t):
            return bank[:, t // 3, (t % 3) * P:(t % 3) * P + P]

        def halves(tile):
            return tile.rearrange("p (a c) -> p a c", a=2)

        x_landed, edges_landed, small_landed = sem("x_landed"), sem("edges_landed"), sem("small_landed")
        raw_landed = [sem(f"raw_landed{i}") for i in range(RAW)]
        const_ready, ident_ready, rstd_ready = sem("const_ready"), sem("ident_ready"), sem("rstd_ready")
        hot_src_ready, hot_dst_ready, endf_ready = sem("hot_src_ready"), sem("hot_dst_ready"), sem("endf_ready")
        xn_ready, var_ready, identr_ready, pick_ready = sem("xn_ready"), sem("var_ready"), sem("identr_ready"), sem("pick_ready")
        xT_psum, xT_f_ready, xT_hi_ready, xT_lo_ready = sem("xT_psum"), sem("xT_f_ready"), sem("xT_hi_ready"), sem("xT_lo_ready")
        count_psum, count_ready = sem("count_psum"), sem("count_ready")
        step_done, hi_done, lo_done = sem("step_done"), sem("hi_done"), sem("lo_done")
        h_hi_done, h_lo_done = sem("h_hi_done"), sem("h_lo_done")
        hT_psum, hT_ready = sem("hT_psum"), sem("hT_ready")
        alpha_psum, diag_ready, row_psum, score_ready = sem("alpha_psum"), sem("diag_ready"), sem("row_psum"), sem("score_ready")
        top_ready, expo_ready, att_ready = sem("top_ready"), sem("expo_ready"), sem("att_ready")
        attT_psum, attT_hi_done, attT_lo_done = sem("attT_psum"), sem("attT_hi_done"), sem("attT_lo_done")
        agg_psum, y_ready, neg_ready, elu_exp_ready = sem("agg_psum"), sem("y_ready"), sem("neg_ready"), sem("elu_exp_ready")
        elu_ready, hid_hi_done, hid_lo_done = sem("elu_ready"), sem("hid_hi_done"), sem("hid_lo_done")
        qkv_ready, qkT_psum, qkT_ready = sem("qkv_ready"), sem("qkT_psum"), sem("qkT_ready")
        feat_psum, feat_ready, kv_psum, kv_ready = sem("feat_psum"), sem("feat_ready"), sem("kv_psum"), sem("kv_ready")
        num_psum, ao_ready, aoT_psum, aoT_hi_done, aoT_lo_done = sem("num_psum"), sem("ao_ready"), sem("aoT_psum"), sem("aoT_hi_done"), sem("aoT_lo_done")
        out_psum, res_ready, ynT_psum, ynT_ready = sem("out_psum"), sem("res_ready"), sem("ynT_psum"), sem("ynT_ready")
        yn_ready, ffn1_psum, gelu_ready, ffn2_psum, fin_ready, stored = sem("yn_ready"), sem("ffn1_psum"), sem("gelu_ready"), sem("ffn2_psum"), sem("fin_ready"), sem("stored")
        dve_chain = sem("dve_chain")

        SMALLS = 9

        def weight_view(u):
            g, j = STEPS[u * STEPS_PER_LOAD]
            kind, n, _ = GROUPS[g]
            table, col = {"head": (w1, n * D), "q": (qkv, 0), "k": (qkv, D), "v": (qkv, 2 * D),
                          "layer2": (w2, 0), "out": (proj, 0)}[kind]
            return table[j * P:(j + STEPS_PER_LOAD) * P, col:col + D].rearrange("(t p) c -> p t c", p=P)

        def raw_of(s):
            u = s // STEPS_PER_LOAD
            return raw[:, u % RAW, s % STEPS_PER_LOAD, :]

        def wait_raw(eng, s):
            u = s // STEPS_PER_LOAD
            eng.wait_ge(raw_landed[u % RAW], 16 * (u // RAW + 1))

        def turn_slot(c):
            return LAST[CHAINS[c][1]] + AT_TURN

        block_ = ctx.enter_context(nc.Block())

        @block_.sync
        def _(sp):
            sp.dma_start(x_sb[:, :], x).then_inc(x_landed, 16)
            for u in range(LOADS):
                if u >= RAW:
                    old = [s for s in range((u - RAW) * STEPS_PER_LOAD, (u - RAW + 1) * STEPS_PER_LOAD)]
                    split = [s for s in old if SPLIT[s]]
                    whole = [s for s in old if not SPLIT[s]]
                    if split:
                        sp.wait_ge(lo_done, SPLITS_BY[split[-1]])
                    if whole:
                        sp.wait_ge(step_done, whole[-1] + 1)
                sp.dma_start(raw[:, u % RAW, :, :], weight_view(u)).then_inc(raw_landed[u % RAW], 16)
            sp.wait_ge(fin_ready, 1)
            sp.dma_start(out, yt[:, :]).then_inc(stored, 16)
            sp.wait_ge(stored, 16)

        @block_.gpsimd
        def _(pool):
            nc.gpsimd.iota(column[:, :], [[1, P]], base=0, channel_multiplier=0,
                           allow_small_or_imprecise_dtypes=True).then_inc(const_ready, 1)
            nc.gpsimd.memset(minus_half[:, :], -0.5).then_inc(const_ready, 1)
            nc.gpsimd.memset(ones[:, :], 1.0).then_inc(const_ready, 1)
            pool.wait_ge(const_ready, 3)
            nc.gpsimd.affine_select(out=ident[:, :], in_=ones[:, :], compare_op=ALU.is_equal, fill=0.0,
                                    base=0, pattern=[[-1, P]], channel_multiplier=1).then_inc(ident_ready, 1)
            pool.wait_ge(var_ready, 1)
            nc.gpsimd.tensor_tensor(rstd[:, :], vpe[:, :], minus_half[:, :], ALU.pow).then_inc(rstd_ready, 1)
            pool.wait_ge(endf_ready, 1)
            for c in range(EC):
                last = nc.gpsimd.tensor_scalar(hot[:, 0, c, :], column[:, :], endf[:, 0, c:c + 1], None, ALU.is_equal)
            last.then_inc(hot_src_ready, 1)
            pool.wait_ge(var_ready, 2)
            nc.gpsimd.tensor_tensor(rstd[:, :], vpe[:, :], minus_half[:, :], ALU.pow).then_inc(rstd_ready, 1)

        @block_.scalar
        def _(act):
            act.dma_start(ends[:, 0, :], src).then_inc(edges_landed, 16)
            act.dma_start(ends[:, 1, :], dst).then_inc(edges_landed, 16)
            for tile, where in ((a1_sb[:, :, :, :], a1), (a2_sb[:, :, :], a2), (b1_sb[:, :, :], b1),
                                (row_sb[:, :], rows), (pm_sb[0:MD, :], pm), (pm_sb[MD:P, :], pm),
                                (w_in_sb[:, :, :], w_in), (b_in_sb[:, :], b_in), (w_out_sb[:, :], w_out)):
                act.dma_start(tile, where).then_inc(small_landed, 16)

            def split_hi(s):
                n = SPLITS_BY[s] - 1
                wait_raw(act, s)
                if n >= PARTS:
                    act.wait_ge(step_done, NTH_SPLIT[n - PARTS] + 1)
                nc.scalar.copy(w_hi[:, n % PARTS, :], raw_of(s)).then_inc(hi_done, 1)

            act.wait_ge(ident_ready, 1)
            nc.scalar.copy(ident_r[:, :], ident[:, :]).then_inc(identr_ready, 1)
            act.wait_ge(xT_psum, 1)
            nc.scalar.copy(halves(xT[:, :, :].rearrange("p t n -> p (t n)")), blocks(wk)).then_inc(xT_f_ready, 1)
            nc.scalar.copy(halves(xT_hi[:, :, :].rearrange("p t n -> p (t n)")), blocks(wk)).then_inc(xT_hi_ready, 1)
            for s in range(LEAD):
                if SPLIT[s]:
                    split_hi(s)

            def take_hi(c):
                g = CHAINS[c][1]
                act.wait_ge(step_done, LAST[g] + 1)
                if c >= 2:
                    act.wait_ge(agg_psum, c - 1)
                nc.scalar.copy(halves(h_hi[:, c % 2, :]), blocks(acc[g % 2])).then_inc(h_hi_done, 1)

            def take_turned(c):
                act.wait_ge(hT_psum, c + 1)
                if c:
                    act.wait_ge(alpha_psum, c)
                nc.scalar.copy(halves(hT[:, :, :].rearrange("p t n -> p (t n)")), blocks(wk)).then_inc(hT_ready, 1)

            def add_scores(c):
                act.wait_ge(row_psum, c + 1)
                act.wait_ge(diag_ready, c + 1)
                nc.scalar.activation(score[:, :], plane[:, 0:P], ACT.Identity, bias=alpha[:, 1:2],
                                     scale=1.0).then_inc(score_ready, 1)

            def exponent(c):
                act.wait_ge(top_ready, c + 1)
                nc.scalar.activation(expo[:, :], masked[:, :], ACT.Exp, bias=ntop[:, 0:1], scale=1.0).then_inc(expo_ready, 1)

            def att_hi(c):
                act.wait_ge(attT_psum, c + 1)
                nc.scalar.copy(attT_hi[:, :], plane[:, P:2 * P]).then_inc(attT_hi_done, 1)

            def elu_exp(c):
                act.wait_ge(y_ready, c + 1)
                if c:
                    act.wait_ge(elu_ready, c)
                nc.scalar.activation(et[:, :], yt[:, :], ACT.Relu, scale=-1.0).then_inc(neg_ready, 1)
                act.wait_ge(neg_ready, c + 1)
                nc.scalar.activation(et[:, :], et[:, :], ACT.Exp, scale=-1.0).then_inc(elu_exp_ready, 1)

            def hidden_hi(c):
                act.wait_ge(elu_ready, c + 1)
                nc.scalar.copy(hid_hi[:, c * TB:(c + 1) * TB, :].rearrange("p t n -> p (t n)"), hf[:, :]).then_inc(hid_hi_done, 1)

            for i in range(len(STEPS)):
                if i + LEAD < len(STEPS) and SPLIT[i + LEAD]:
                    split_hi(i + LEAD)
                for c, g in CHAINS:
                    e = LAST[g]
                    late = c == HEADS
                    if i == e:
                        take_hi(c)
                    if i == e + AT_TURN:
                        take_turned(c)
                    if i == e + (TAIL_ROW if late else AT_ROW):
                        add_scores(c)
                        exponent(c)
                    if i == e + (TAIL_ATT if late else AT_ATT):
                        att_hi(c)
                    if not late and i == e + AT_AGG:
                        elu_exp(c)
                    if not late and i == e + AT_ELU:
                        hidden_hi(c)
                for n, g in enumerate((G_Q, G_K)):
                    if i == LAST[g]:
                        act.wait_ge(step_done, LAST[g] + 1)
                        if n:
                            act.wait_ge(qkT_psum, 1)
                        nc.scalar.copy(halves(qk[:, :]), blocks(acc[g % 2])).then_inc(qkv_ready, 1)
                    if i == LAST[g] + 2:
                        act.wait_ge(qkT_psum, n + 1)
                        nc.scalar.copy(halves((qT, kT)[n].rearrange("p t n -> p (t n)")), blocks(wk)).then_inc(qkT_ready, 1)
                if i == LAST[G_V]:
                    act.wait_ge(step_done, LAST[G_V] + 1)
                    for a in range(2):
                        last = nc.scalar.copy(v1[:, a * 6:a * 6 + 6, 0:MD],
                                              acc[G_V % 2][:, a, 0:HALF].rearrange("p (h d) -> p h d", d=MD))
                    last.then_inc(qkv_ready, 1)
                if i == AT_AO:
                    act.wait_ge(aoT_psum, 1)
                    nc.scalar.copy(halves(h_hi[:, 1, :]), blocks(wk)).then_inc(aoT_hi_done, 1)

            act.wait_ge(ynT_psum, 1)
            nc.scalar.copy(halves(hT[:, :, :].rearrange("p t n -> p (t n)")), blocks(wk)).then_inc(ynT_ready, 1)
            act.wait_ge(ffn1_psum, 1)
            nc.scalar.activation(f_hid[:, :], small[0:HID, 0:P], ACT.Gelu, bias=b_in_sb[:, 0:1], scale=1.0).then_inc(gelu_ready, 1)

        @block_.vector
        def _(dve):
            chain = [0]

            def link(ins):
                chain[0] += 1
                ins.then_inc(dve_chain, 1)
                dve.wait_ge(dve_chain, chain[0])

            def norm(tile, to, n, ready):
                for a in range(2):
                    last = nc.vector.bn_stats(stats[:, a, :], tile[:, a * HALF:(a + 1) * HALF])
                link(last)
                link(nc.vector.bn_aggr(mv[:, :], stats[:, :, :]))
                nc.vector.tensor_scalar(vpe[:, :], mv[:, 1:2], LN_EPS, None, ALU.add).then_inc(var_ready, 1)
                dve.wait_ge(rstd_ready, n)
                nc.vector.tensor_scalar(to, tile, mv[:, 0:1], rstd[:, 0:1], ALU.subtract, ALU.mult).then_inc(ready, 1)

            dve.wait_ge(x_landed, 16)
            norm(x_sb[:, :], xn[:, :], 1, xn_ready)
            dve.wait_ge(edges_landed, 32)
            nc.vector.tensor_copy(endf[:, :, :], ends[:, :, :]).then_inc(endf_ready, 1)
            dve.wait_ge(endf_ready, 1)
            dve.wait_ge(const_ready, 3)
            dve.wait_ge(xT_hi_ready, 1)
            nc.vector.tensor_tensor(halves(xT_lo[:, :, :].rearrange("p t n -> p (t n)")), blocks(wk),
                                    halves(xT_hi[:, :, :].rearrange("p t n -> p (t n)").bitcast(F32)),
                                    ALU.subtract).then_inc(xT_lo_ready, 1)
            for c in range(EC):
                last = nc.vector.tensor_scalar(hot[:, 1, c, :], column[:, :], endf[:, 1, c:c + 1], None, ALU.is_equal)
            last.then_inc(hot_dst_ready, 1)

            def split_lo(s):
                n = SPLITS_BY[s] - 1
                dve.wait_ge(hi_done, n + 1)
                nc.vector.tensor_tensor(w_lo[:, n % PARTS, :], raw_of(s), w_hi[:, n % PARTS, :].bitcast(F32),
                                        ALU.subtract).then_inc(lo_done, 1)

            for s in range(LEAD):
                if SPLIT[s]:
                    split_lo(s)

            def counts():
                dve.wait_ge(count_psum, 1)
                link(nc.vector.tensor_copy(count[:, :], small[:, 0:P]))
                link(nc.vector.tensor_scalar(absent[:, :], count[:, :], 1.0, 1.0, ALU.min, ALU.subtract))
                nc.vector.tensor_scalar(absent[:, :], absent[:, :], FAR, None, ALU.mult).then_inc(count_ready, 1)
                dve.wait_ge(small_landed, 16 * SMALLS)
                nc.vector.tensor_scalar(pm_sb[:, :], pm_sb[:, :], float(MF) ** -0.5, None, ALU.mult)
                dve.wait_ge(ident_ready, 1)
                for r in range(4):
                    last = nc.vector.tensor_scalar(pick[:, r, :], ones[0:5, :], ident[0:5, r:r + 1], None, ALU.mult)
                link(last)
                nc.vector.tensor_scalar(pick[:, 3, :], pick[:, 3, :], ident[0:5, 4:5], None, ALU.add).then_inc(pick_ready, 1)
                dve.wait_ge(pick_ready, 1)
                dve.wait_ge(count_ready, 1)

            def take_lo(c):
                g = CHAINS[c][1]
                dve.wait_ge(h_hi_done, c + 1)
                nc.vector.tensor_tensor(halves(h_lo[:, c % 2, :]), blocks(acc[g % 2]),
                                        halves(h_hi[:, c % 2, :].bitcast(F32)), ALU.subtract).then_inc(h_lo_done, 1)

            def scores(c):
                dve.wait_ge(alpha_psum, c + 1)
                if c:
                    dve.wait_ge(score_ready, c)
                link(nc.vector.tensor_copy(alpha[:, :], small[:, 0:2]))
                nc.vector.tensor_scalar(diag[:, :], ident[:, :], alpha[:, 0:1], None, ALU.mult).then_inc(diag_ready, 1)

            def maximum(c):
                dve.wait_ge(score_ready, c + 1)
                link(nc.vector.scalar_tensor_tensor(out=leaky[:, :], in0=score[:, :], scalar=SLOPE, in1=score[:, :],
                                                    op0=ALU.mult, op1=ALU.max))
                link(nc.vector.tensor_tensor_reduce(out=masked[:, :], in0=leaky[:, :], in1=absent[:, :], scale=1.0,
                                                    scalar=-3e38, op0=ALU.add, op1=ALU.max, accum_out=top[:, :]))
                nc.vector.tensor_scalar(ntop[:, :], top[:, :], -1.0, None, ALU.mult).then_inc(top_ready, 1)

            def normalise(c):
                dve.wait_ge(expo_ready, c + 1)
                link(nc.vector.tensor_tensor_reduce(out=weight[:, :], in0=expo[:, :], in1=count[:, :], scale=1.0,
                                                    scalar=0.0, op0=ALU.mult, op1=ALU.add, accum_out=den[:, :]))
                link(nc.vector.tensor_scalar(dene[:, :], den[:, :], DENOM_EPS, None, ALU.add))
                link(nc.vector.reciprocal(rden[:, :], dene[:, :]))
                nc.vector.tensor_scalar(att[:, :], weight[:, :], rden[:, 0:1], None, ALU.mult).then_inc(att_ready, 1)

            def att_lo(c):
                dve.wait_ge(attT_hi_done, c + 1)
                nc.vector.tensor_tensor(attT_lo[:, :], plane[:, P:2 * P], attT_hi[:, :].bitcast(F32),
                                        ALU.subtract).then_inc(attT_lo_done, 1)

            def add_b1(c):
                dve.wait_ge(agg_psum, c + 1)
                if c == 0:
                    dve.wait_ge(small_landed, 16 * SMALLS)
                for a in range(2):
                    last = nc.vector.tensor_tensor(
                        yt[:, a * HALF:(a + 1) * HALF].rearrange("p (t n) -> p t n", n=P),
                        wk[:, a, 0:HALF].rearrange("p (t n) -> p t n", n=P),
                        b1_sb[:, c, 3 * a:3 * a + 3].unsqueeze(2).broadcast_to([P, 3, P]), ALU.add)
                last.then_inc(y_ready, 1)

            def elu(c):
                dve.wait_ge(elu_exp_ready, c + 1)
                if c:
                    dve.wait_ge(hid_hi_done, c)
                nc.vector.scalar_tensor_tensor(out=hf[:, :], in0=et[:, :], scalar=-1.0, in1=yt[:, :],
                                               op0=ALU.add, op1=ALU.max).then_inc(elu_ready, 1)

            def hidden_lo(c):
                dve.wait_ge(hid_hi_done, c + 1)
                at = slice(c * TB, (c + 1) * TB)
                nc.vector.tensor_tensor(hid_lo[:, at, :].rearrange("p t n -> p (t n)"), hf[:, :],
                                        hid_hi[:, at, :].rearrange("p t n -> p (t n)").bitcast(F32),
                                        ALU.subtract).then_inc(hid_lo_done, 1)

            def features(t):
                dve.wait_ge(feat_psum, t + 1)
                if t:
                    dve.wait_ge(num_psum, t)
                nc.vector.tensor_scalar(feats, wk[:, :, :], FEATURE_EPS, FEATURE_EPS, ALU.add, ALU.max).then_inc(feat_ready, 1)

            def keep_kv(t):
                dve.wait_ge(kv_psum, t + 1)
                nc.vector.tensor_copy(kv[:, :, :].rearrange("p a d -> p (a d)"), small[:, 0:4 * (MD + 1)]).then_inc(kv_ready, 1)

            def divide(t):
                dve.wait_ge(num_psum, t + 1)
                both = plane[:, 0:2 * (MD + 1)].rearrange("p (h d) -> p h d", h=2)
                link(nc.vector.reciprocal(mrec[:, :], both[:, :, MD]))
                nc.vector.tensor_tensor(ao[:, t * PAIR:(t + 1) * PAIR].rearrange("p (h d) -> p h d", h=2),
                                        both[:, :, 0:MD], mrec[:, :].unsqueeze(2).broadcast_to([P, 2, MD]),
                                        ALU.mult).then_inc(ao_ready, 1)

            for i in range(len(STEPS)):
                if i + LEAD < len(STEPS) and SPLIT[i + LEAD]:
                    split_lo(i + LEAD)
                if i == 3:
                    counts()
                if i == FIRST[G_V]:
                    dve.wait_ge(count_psum, 1)
                    nc.vector.memset(v1[:, :, MD:MD + 1], 1.0)
                for c, g in CHAINS:
                    e = LAST[g]
                    late = c == HEADS
                    if i == e:
                        take_lo(c)
                    if i == e + (TAIL_ALPHA if late else AT_ALPHA):
                        scores(c)
                    if i == e + (TAIL_ROW if late else AT_ROW):
                        maximum(c)
                        normalise(c)
                    if i == e + (TAIL_ATT if late else AT_ATT):
                        att_lo(c)
                    if not late and i == e + AT_AGG:
                        add_b1(c)
                    if not late and i == e + AT_ELU:
                        elu(c)
                        hidden_lo(c)
                for t in range(TB):
                    at = PAIR_FIRST + PAIR_EVERY * t
                    if i == at:
                        features(t)
                    if i == at + 2:
                        keep_kv(t)
                    if i == at + 4:
                        divide(t)
                if i == AT_AO:
                    dve.wait_ge(aoT_hi_done, 1)
                    nc.vector.tensor_tensor(halves(h_lo[:, 1, :]), blocks(wk), halves(h_hi[:, 1, :].bitcast(F32)),
                                            ALU.subtract).then_inc(aoT_lo_done, 1)

            dve.wait_ge(out_psum, 1)
            link(nc.vector.tensor_tensor(halves(x_sb[:, :]), blocks(acc[G_OUT % 2]), halves(x_sb[:, :]), ALU.add))
            norm(x_sb[:, :], hf[:, :], 2, yn_ready)
            dve.wait_ge(ffn2_psum, 1)
            nc.vector.tensor_tensor(halves(yt[:, :]), blocks(acc[1 - G_OUT % 2]), halves(x_sb[:, :]), ALU.add).then_inc(fin_ready, 1)

        @block_.tensor
        def _(pe):
            def turn(tile, t0=0):
                for t in range(TB):
                    last = nc.tensor.transpose(block(wk, t), tile[:, t * P:(t + 1) * P], ident[:, :])
                return last

            pe.wait_ge(xn_ready, 1)
            pe.wait_ge(ident_ready, 1)
            turn(xn).then_inc(xT_psum, 1)

            def stationary(s):
                g, j = STEPS[s]
                kind = GROUPS[g][0]
                if kind == "layer2":
                    return None, hid_hi[:, j, :], hid_lo[:, j, :]
                if kind == "out":
                    cols = slice(j * P, (j + 1) * P)
                    return None, h_hi[:, 1, cols], h_lo[:, 1, cols]
                return xT[:, j, :], xT_hi[:, j, :], xT_lo[:, j, :]

            def open_group(g):
                bank = acc[g % 2]
                if 2 <= g <= HEADS + 1:
                    pe.wait_ge(h_lo_done, g - 1)
                if g >= G_V:
                    pe.wait_ge(qkv_ready, g - G_V + 1)
                rows_of = {G_Q: 0, G_K: 1, G_V: 2, G_OUT: 3}
                if g in rows_of:
                    pe.wait_ge(pick_ready, 1)
                    for a in range(2):
                        nc.tensor.matmul(bank[:, a, 0:HALF], pick[:, rows_of[g], :],
                                         row_sb[:, a * HALF:(a + 1) * HALF], start=True, stop=False)

            def step(s):
                g, j = STEPS[s]
                bank = acc[g % 2]
                opens = j == 0 and g not in (G_Q, G_K, G_V, G_OUT)
                closes = j == GROUPS[g][2] - 1 and g != G_OUT
                if j == 0:
                    open_group(g)
                if g == 0 and j == 0:
                    pe.wait_ge(xT_f_ready, 1)
                if s == NTH_SPLIT[0]:
                    pe.wait_ge(xT_lo_ready, 1)
                if g == G_L2 and j % TB == 0:
                    pe.wait_ge(hid_lo_done, j // TB + 1)
                if g == G_OUT and j == 0:
                    pe.wait_ge(aoT_lo_done, 1)
                full, hi, lo = stationary(s)
                if SPLIT[s]:
                    n = SPLITS_BY[s] - 1
                    pe.wait_ge(lo_done, n + 1)
                    passes = [(hi, w_hi[:, n % PARTS, :]), (hi, w_lo[:, n % PARTS, :]), (lo, w_hi[:, n % PARTS, :])]
                else:
                    wait_raw(pe, s)
                    passes = [(full, raw_of(s))]
                for k, (left, right) in enumerate(passes):
                    for a in range(2):
                        last = nc.tensor.matmul(bank[:, a, 0:HALF], left, right[:, a * HALF:(a + 1) * HALF],
                                                start=opens and k == 0, stop=closes and k == len(passes) - 1)
                last.then_inc(step_done, 1)

            def count_edges():
                pe.wait_ge(hot_src_ready, 1)
                pe.wait_ge(hot_dst_ready, 1)
                for c in range(EC):
                    last = nc.tensor.matmul(small[:, 0:P], hot[:, 1, c, :], hot[:, 0, c, :],
                                            start=(c == 0), stop=(c == EC - 1))
                last.then_inc(count_psum, 1)

            def turn_head(c):
                pe.wait_ge(h_lo_done, c + 1)
                if c == 0:
                    pe.wait_ge(identr_ready, 1)
                    pe.wait_ge(xT_lo_ready, 1)
                if 2 <= c < HEADS:
                    pe.wait_ge(y_ready, c - 1)
                if c == HEADS:
                    pe.wait_ge(aoT_lo_done, 1)
                for t in range(TB):
                    cols = slice(t * P, (t + 1) * P)
                    nc.tensor.matmul(block(wk, t), h_hi[:, c % 2, cols], ident_r[:, :], start=True, stop=False)
                    last = nc.tensor.matmul(block(wk, t), h_lo[:, c % 2, cols], ident_r[:, :], start=False, stop=True)
                last.then_inc(hT_psum, 1)

            def alphas(c):
                pe.wait_ge(hT_ready, c + 1)
                if c == 0:
                    pe.wait_ge(small_landed, 16 * SMALLS)
                    pe.wait_ge(count_ready, 1)
                if c == HEADS:
                    pe.wait_ge(kv_ready, TB)
                for t in range(TB):
                    vec = a2_sb[:, t, :] if c == HEADS else a1_sb[:, c, t, :]
                    last = nc.tensor.matmul(small[:, 0:2], hT[:, t, :], vec, start=(t == 0), stop=(t == TB - 1))
                last.then_inc(alpha_psum, 1)

            def source_rows(c):
                pe.wait_ge(diag_ready, c + 1)
                if c:
                    pe.wait_ge(attT_lo_done, c)
                nc.tensor.matmul(plane[:, 0:P], ones[:, :], diag[:, :], start=True, stop=True).then_inc(row_psum, 1)

            def turn_att(c):
                pe.wait_ge(att_ready, c + 1)
                nc.tensor.transpose(plane[:, P:2 * P], att[:, :], ident[:, :]).then_inc(attT_psum, 1)

            def aggregate(c):
                pe.wait_ge(attT_lo_done, c + 1)
                pe.wait_ge(hT_ready, min(c + 2, HEADS))
                if c == HEADS - 1:
                    pe.wait_ge(qkT_ready, 1)
                for t in range(TB):
                    cols = slice(t * P, (t + 1) * P)
                    nc.tensor.matmul(block(wk, t), h_hi[:, c % 2, cols], attT_hi[:, :], start=True, stop=False)
                    nc.tensor.matmul(block(wk, t), h_hi[:, c % 2, cols], attT_lo[:, :], start=False, stop=False)
                    last = nc.tensor.matmul(block(wk, t), h_lo[:, c % 2, cols], attT_hi[:, :], start=False, stop=True)
                last.then_inc(agg_psum, 1)

            def pair_features(t):
                if t == 0:
                    pe.wait_ge(qkT_ready, 2)
                    pe.wait_ge(y_ready, HEADS)
                for h in range(2):
                    rows_ = slice(h * MD, (h + 1) * MD)
                    nc.tensor.matmul(wk[:, h, 0:MF], kT[rows_, t, :], pm_sb[rows_, :], start=True, stop=True)
                    for m in range(2):
                        last = nc.tensor.matmul(wk[:, h, MF + m * P:MF + (m + 1) * P], pm_sb[rows_, m * P:(m + 1) * P],
                                                qT[rows_, t, :], start=True, stop=True)
                last.then_inc(feat_psum, 1)

            def pair_kv(t):
                pe.wait_ge(feat_ready, t + 1)
                if t == 0:
                    pe.wait_ge(qkv_ready, 3)
                for h in range(2):
                    for m in range(2):
                        at = (2 * h + m) * (MD + 1)
                        last = nc.tensor.matmul(small[:, at:at + MD + 1], feats[:, h, m * P:(m + 1) * P],
                                                v1[:, 2 * t + h, :], start=True, stop=True)
                last.then_inc(kv_psum, 1)

            def pair_num(t):
                pe.wait_ge(kv_ready, t + 1)
                if t:
                    pe.wait_ge(ao_ready, t)
                for h in range(2):
                    for m in range(2):
                        last = nc.tensor.matmul(plane[:, h * (MD + 1):(h + 1) * (MD + 1)],
                                                feats[:, h, MF + m * P:MF + (m + 1) * P], kv[:, 2 * h + m, :],
                                                start=(m == 0), stop=(m == 1))
                last.then_inc(num_psum, 1)

            for i in range(len(STEPS)):
                step(i)
                if i == 2:
                    count_edges()
                for n, g in enumerate((G_Q, G_K)):
                    if i == LAST[g] + 2:
                        pe.wait_ge(qkv_ready, n + 1)
                        pe.wait_ge(y_ready, HEADS - 1 + n)
                        turn(qk).then_inc(qkT_psum, 1)
                for c, g in CHAINS:
                    e = LAST[g]
                    late = c == HEADS
                    if i == e + AT_TURN:
                        turn_head(c)
                    if i == e + (TAIL_ALPHA if late else AT_ALPHA):
                        alphas(c)
                    if i == e + (TAIL_ROW if late else AT_ROW):
                        source_rows(c)
                    if i == e + (TAIL_ATT if late else AT_ATT):
                        turn_att(c)
                    if not late and i == e + AT_AGG:
                        aggregate(c)
                for t in range(TB):
                    at = PAIR_FIRST + PAIR_EVERY * t
                    if i == at:
                        pair_features(t)
                    if i == at + 2:
                        pair_kv(t)
                    if i == at + 4:
                        pair_num(t)
                if i == AT_AO:
                    pe.wait_ge(ao_ready, TB)
                    turn(ao).then_inc(aoT_psum, 1)

            pe.wait_ge(attT_lo_done, HEADS + 1)
            pairs = [(attT_hi, h_hi), (attT_hi, h_lo), (attT_lo, h_hi)]
            for k, (left, right) in enumerate(pairs):
                for a in range(2):
                    last = nc.tensor.matmul(acc[G_OUT % 2][:, a, 0:HALF], left[:, :],
                                            right[:, 0, a * HALF:(a + 1) * HALF], start=False, stop=(k == 2))
            last.then_inc(out_psum, 1)

            pe.wait_ge(yn_ready, 1)
            turn(hf).then_inc(ynT_psum, 1)
            pe.wait_ge(ynT_ready, 1)
            for t in range(TB):
                last = nc.tensor.matmul(small[0:HID, 0:P], w_in_sb[:, t, :], hT[:, t, :],
                                        start=(t == 0), stop=(t == TB - 1))
            last.then_inc(ffn1_psum, 1)
            pe.wait_ge(gelu_ready, 1)
            for a in range(2):
                last = nc.tensor.matmul(acc[1 - G_OUT % 2][:, a, 0:HALF], f_hid[:, :],
                                        w_out_sb[:, a * HALF:(a + 1) * HALF], start=True, stop=True)
            last.then_inc(ffn2_psum, 1)


def kernel(x, src, dst, L0_gnn_W1, L0_gnn_a_src1, L0_gnn_a_dst1, L0_gnn_b1, L0_gnn_W2, L0_gnn_a_src2,
           L0_gnn_a_dst2, L0_gnn_b2, L0_mix_qkv_w, L0_mix_qkv_b, L0_mix_proj_w, L0_mix_proj_b,
           L0_mix_proj_mat, L0_ffn_in_weight, L0_ffn_in_bias, L0_ffn_out_weight):
    import numpy as np
    import concourse.bacc as bacc
    from concourse.bass_utils import run_bass_kernel_spmd

    def by_partition(a):
        a = np.asarray(a)
        return np.ascontiguousarray(np.moveaxis(a.reshape(*a.shape[:-1], TB, P), -1, 0))

    qkv_b = np.asarray(L0_mix_qkv_b).reshape(3, D)
    arrays = {
        "x": np.asarray(x),
        "src": np.asarray(src).reshape(P, EC),
        "dst": np.asarray(dst).reshape(P, EC),
        "w1": np.asarray(L0_gnn_W1),
        "w2": np.asarray(L0_gnn_W2),
        "qkv": np.asarray(L0_mix_qkv_w).T,
        "proj": np.asarray(L0_mix_proj_w).T,
        "a1": np.stack([by_partition(L0_gnn_a_src1), by_partition(L0_gnn_a_dst1)], axis=-1),
        "a2": np.stack([by_partition(L0_gnn_a_src2)[:, 0], by_partition(L0_gnn_a_dst2)[:, 0]], axis=-1),
        "b1": by_partition(np.asarray(L0_gnn_b1).reshape(HEADS, D)),
        "rows": np.concatenate([qkv_b, np.asarray(L0_mix_proj_b)[None], np.asarray(L0_gnn_b2)[None]]),
        "pm": np.asarray(L0_mix_proj_mat).T,
        "w_in": np.moveaxis(by_partition(L0_ffn_in_weight), 1, 2),
        "b_in": np.asarray(L0_ffn_in_bias).reshape(HID, 1),
        "w_out": np.asarray(L0_ffn_out_weight),
    }
    arrays = {f"in_{n}_dram": np.ascontiguousarray(a) for n, a in arrays.items()}
    nc = bacc.Bacc("TRN2", target_bir_lowering=False, num_devices=1)
    args = [nc.dram_tensor(n, a.shape, mybir.dt.from_np(a.dtype), kind="ExternalInput").ap()
            for n, a in arrays.items()]
    args.append(nc.dram_tensor("out_0_dram", (P, D), F32, kind="ExternalOutput").ap())
    build_gps_layer(nc, *args)
    r = run_bass_kernel_spmd(nc, [arrays], core_ids=[0])
    return r.results[0]["out_0_dram"]
```

```python
from contextlib import ExitStack

import concourse.bass as bass
from concourse import mybir

ALU = mybir.AluOpType
ACT = mybir.ActivationFunctionType
F32 = mybir.dt.float32
F32R = mybir.dt.float32r
BF16 = mybir.dt.bfloat16
I32 = mybir.dt.int32

P = 128
D = 768
HEADS = 8
TB = D // P
HALF = D // 2
EDGES = 4096
EC = EDGES // P
MH, MD = 12, 64
MF = 256
PAIR = 2 * MD
HID = 48
LN_EPS = 1e-5
FEATURE_EPS = 1e-3
DENOM_EPS = 1e-16
SLOPE = 0.2
FAR = 1e30

STEPS_PER_LOAD = 3
GROUPS = ([("head", h, TB) for h in range(HEADS)] + [("q", 0, TB), ("k", 1, TB), ("v", 2, TB)]
          + [("layer2", 0, HEADS * TB), ("out", 0, TB)])
STEPS = [(g, j) for g, (_, _, n) in enumerate(GROUPS) for j in range(n)]
G_Q, G_K, G_V, G_L2, G_OUT = range(HEADS, HEADS + 5)
FIRST = [sum(n for _, _, n in GROUPS[:g]) for g in range(len(GROUPS))]
LAST = [sum(n for _, _, n in GROUPS[:g + 1]) - 1 for g in range(len(GROUPS))]
LOADS = len(STEPS) // STEPS_PER_LOAD
RAW = 4
PARTS = 7
LEAD_HI, LEAD_LO = 6, 5

WHOLE = (2,)
SPLIT = [g >= HEADS or (s >= 4 and s % 6 not in WHOLE) for s, (g, _) in enumerate(STEPS)]
SPLITS_BY = [sum(SPLIT[:s + 1]) for s in range(len(STEPS))]
NTH_SPLIT = [s for s in range(len(STEPS)) if SPLIT[s]]

CHAINS = [(c, c) for c in range(HEADS)] + [(HEADS, G_L2)]
STAGES = ("take turn turned alphas scores row add_scores maximum exponent normalise "
          "turn_att turned_att aggregate add_b1 elu_exp elu hidden_hi hidden_lo").split()
HEAD_AT = dict(zip(STAGES, (0, 2, 2, 4, 5, 5, 6, 7, 7, 8, 9, 9, 10, 11, 12, 13, 16, 17)))
TAIL_AT = dict(zip(STAGES, (0, 1, 2, 2, 2, 2, 2, 2, 2, 3, 5, 4)))


def stages_at(i):
    return [(name, c) for c, g in CHAINS for name, k in (TAIL_AT if c == HEADS else HEAD_AT).items()
            if i == LAST[g] + k]


AGG_FIRST = HEAD_AT["aggregate"] < TB + HEAD_AT["turn"]

QK_TAKE, QK_TURN, QK_TURNED, V_TAKE = 0, 2, 2, 3
Q_FIRST = LAST[G_Q] + QK_TURN <= LAST[HEADS - 1] + HEAD_AT["aggregate"]
PAIR_FIRST = FIRST[G_L2] + 0
PAIR_EVERY = 5
PAIR_AT = dict(zip("pair_features features pair_kv keep_kv pair_num divide".split(), (0, 0, 3, 3, 4, 4)))
AO_TURN, AO_HI, AO_LO = (PAIR_FIRST + PAIR_EVERY * TB + k for k in (0, 0, 0))
COUNT_AT, COUNTED_AT = 2, 2


def pairs_at(i):
    return [(name, t) for t in range(TB) for name, k in PAIR_AT.items() if i == PAIR_FIRST + PAIR_EVERY * t + k]


def build_gps_layer(nc, x, src, dst, w1, w2, qkv, proj, a1, a2, b1, rows, pm, w_in, b_in, w_out, out):
    ctx = ExitStack()
    with ctx:
        def sb(name, shape, dt=F32):
            return ctx.enter_context(nc.sbuf_tensor(name, shape, dt))

        def ps(name, shape):
            return ctx.enter_context(nc.psum_tensor(name, shape, F32))

        def sem(name):
            return ctx.enter_context(nc.semaphore(name))

        raw = sb("raw", [P, RAW, STEPS_PER_LOAD, D])
        w_hi = sb("w_hi", [P, PARTS, D], F32R)
        w_lo = sb("w_lo", [P, PARTS, D], F32R)
        hid_hi = sb("hid_hi", [P, HEADS * TB, P], F32R)
        hid_lo = sb("hid_lo", [P, HEADS * TB, P], F32R)
        xT = sb("xT", [P, TB, P])
        xT_hi = sb("xT_hi", [P, TB, P], F32R)
        xT_lo = sb("xT_lo", [P, TB, P], F32R)
        x_sb = sb("x_sb", [P, D])
        h = sb("h", [P, 2, D])
        ao_hi = sb("ao_hi", [P, D], F32R)
        ao_lo = sb("ao_lo", [P, D], F32R)
        hT = sb("hT", [P, TB, P])
        yt = sb("yt", [P, D])
        et = sb("et", [P, D])
        hf = sb("hf", [P, D])
        scratch = sb("scratch", [P, 4176])
        qk = sb("qk", [P, D])
        count = sb("count", [P, P])
        absent = sb("absent", [P, P])
        score = sb("score", [P, P])
        leaky = sb("leaky", [P, P])
        masked = sb("masked", [P, P])
        expo = sb("expo", [P, P])
        weight = sb("weight", [P, P])
        att = sb("att", [P, P])
        diag = sb("diag", [P, P])
        ident = sb("ident", [P, P])
        ones = sb("ones", [P, P])
        column = sb("column", [P, P], BF16)
        attT = sb("attT", [P, P])
        row_sb = sb("row_sb", [5, D])
        row_hi = sb("row_hi", [5, D], F32R)
        row_lo = sb("row_lo", [5, D], F32R)
        pick = sb("pick", [5, 4, P], F32R)
        pm_sb = sb("pm_sb", [P, MF])
        a1_sb = sb("a1_sb", [P, HEADS, TB, 2])
        a2_sb = sb("a2_sb", [P, TB, 2])
        b1_sb = sb("b1_sb", [P, HEADS, TB])
        w_in_sb = sb("w_in_sb", [P, TB, HID])
        b_in_sb = sb("b_in_sb", [HID, 1])
        w_out_sb = sb("w_out_sb", [HID, D])
        f_hid = sb("f_hid", [HID, P])
        ends = sb("ends", [P, 2, EC], I32)
        endf = sb("endf", [P, 2, EC])
        kv = sb("kv", [P, 4, MD + 1])
        alpha = sb("alpha", [P, 2])
        stats = sb("stats", [P, 2, 6])
        mv = sb("mv", [P, 2])
        vpe = sb("vpe", [P, 1])
        rstd = sb("rstd", [P, 1])
        minus_half = sb("minus_half", [P, 1])
        top = sb("top", [P, 1])
        ntop = sb("ntop", [P, 1])
        den = sb("den", [P, 1])
        dene = sb("dene", [P, 1])
        rden = sb("rden", [P, 1])
        mrec = sb("mrec", [P, 2])

        hot = scratch[:, 0:2 * EC * P // 2].bitcast(BF16).rearrange("p (a c n) -> p a c n", a=2, c=EC)
        qT = scratch[:, 0:D].rearrange("p (t n) -> p t n", t=TB)
        kT = scratch[:, D:2 * D].rearrange("p (t n) -> p t n", t=TB)
        v1 = scratch[:, 2 * D:2 * D + MH * (MD + 1)].rearrange("p (h d) -> p h d", h=MH)
        AO0 = 2 * D + MH * (MD + 1)
        ao = scratch[:, AO0:AO0 + D]
        feats = scratch[:, AO0 + D:AO0 + D + 1024].rearrange("p (a f) -> p a f", a=2)
        xn = hf

        acc = [ps(f"acc{i}", [P, 2, 512]) for i in range(2)]
        wk = ps("wk", [P, 2, 512])
        small = ps("small", [P, 512])
        plane = ps("plane", [P, 512])

        def blocks(bank):
            return bank[:, :, 0:HALF]

        def block(bank, t):
            return bank[:, t // 3, (t % 3) * P:(t % 3) * P + P]

        def halves(tile):
            return tile.rearrange("p (a c) -> p a c", a=2)

        x_landed, edges_landed, small_landed = sem("x_landed"), sem("edges_landed"), sem("small_landed")
        raw_landed = [sem(f"raw_landed{i}") for i in range(RAW)]
        const_ready, ident_ready, rstd_ready = sem("const_ready"), sem("ident_ready"), sem("rstd_ready")
        hot_ready, endf_ready = sem("hot_ready"), sem("endf_ready")
        xn_ready, var_ready, pick_ready = sem("xn_ready"), sem("var_ready"), sem("pick_ready")
        xT_psum, xT_f_ready, xT_hi_ready, xT_lo_ready = sem("xT_psum"), sem("xT_f_ready"), sem("xT_hi_ready"), sem("xT_lo_ready")
        count_psum, count_ready = sem("count_psum"), sem("count_ready")
        step_done, hi_done, lo_done = sem("step_done"), sem("hi_done"), sem("lo_done")
        h_ready = sem("h_ready")
        hT_psum, hT_ready = sem("hT_psum"), sem("hT_ready")
        alpha_psum, diag_ready, row_psum, score_ready = sem("alpha_psum"), sem("diag_ready"), sem("row_psum"), sem("score_ready")
        top_ready, expo_ready, att_ready = sem("top_ready"), sem("expo_ready"), sem("att_ready")
        attT_psum, attT_ready, row_hi_ready = sem("attT_psum"), sem("attT_ready"), sem("row_hi_ready")
        agg_psum, y_ready, neg_ready, elu_exp_ready = sem("agg_psum"), sem("y_ready"), sem("neg_ready"), sem("elu_exp_ready")
        elu_ready, hid_hi_done, hid_lo_done = sem("elu_ready"), sem("hid_hi_done"), sem("hid_lo_done")
        qkv_ready, qkT_psum, qkT_ready = sem("qkv_ready"), sem("qkT_psum"), sem("qkT_ready")
        feat_psum, feat_ready, kv_psum, kv_ready = sem("feat_psum"), sem("feat_ready"), sem("kv_psum"), sem("kv_ready")
        num_psum, ao_ready, aoT_psum, aoT_hi_done, aoT_lo_done = sem("num_psum"), sem("ao_ready"), sem("aoT_psum"), sem("aoT_hi_done"), sem("aoT_lo_done")
        out_psum, res_ready, ynT_psum, ynT_ready = sem("out_psum"), sem("res_ready"), sem("ynT_psum"), sem("ynT_ready")
        yn_ready, ffn1_psum, gelu_ready, ffn2_psum, fin_ready, stored = sem("yn_ready"), sem("ffn1_psum"), sem("gelu_ready"), sem("ffn2_psum"), sem("fin_ready"), sem("stored")
        dve_chain = sem("dve_chain")

        SMALLS = 9

        def weight_view(u):
            g, j = STEPS[u * STEPS_PER_LOAD]
            kind, n, _ = GROUPS[g]
            table, col = {"head": (w1, n * D), "q": (qkv, 0), "k": (qkv, D), "v": (qkv, 2 * D),
                          "layer2": (w2, 0), "out": (proj, 0)}[kind]
            return table[j * P:(j + STEPS_PER_LOAD) * P, col:col + D].rearrange("(t p) c -> p t c", p=P)

        def raw_of(s):
            u = s // STEPS_PER_LOAD
            return raw[:, u % RAW, s % STEPS_PER_LOAD, :]

        def wait_raw(eng, s):
            u = s // STEPS_PER_LOAD
            eng.wait_ge(raw_landed[u % RAW], 16 * (u // RAW + 1))

        block_ = ctx.enter_context(nc.Block())

        @block_.sync
        def _(sp):
            sp.dma_start(x_sb[:, :], x).then_inc(x_landed, 16)
            sp.dma_start(ends[:, 0, :], src).then_inc(edges_landed, 16)
            sp.dma_start(ends[:, 1, :], dst).then_inc(edges_landed, 16)
            smalls = [(a1_sb[:, :, :, :], a1), (a2_sb[:, :, :], a2), (b1_sb[:, :, :], b1),
                      (row_sb[:, :], rows), (pm_sb[0:MD, :], pm), (pm_sb[MD:P, :], pm),
                      (w_in_sb[:, :, :], w_in), (b_in_sb[:, :], b_in), (w_out_sb[:, :], w_out)]
            for u in range(LOADS):
                if u >= RAW:
                    old = [s for s in range((u - RAW) * STEPS_PER_LOAD, (u - RAW + 1) * STEPS_PER_LOAD)]
                    split = [s for s in old if SPLIT[s]]
                    whole = [s for s in old if not SPLIT[s]]
                    if split:
                        sp.wait_ge(lo_done, SPLITS_BY[split[-1]])
                    if whole:
                        sp.wait_ge(step_done, whole[-1] + 1)
                sp.dma_start(raw[:, u % RAW, :, :], weight_view(u)).then_inc(raw_landed[u % RAW], 16)
                if u == 2:
                    for tile, where in smalls:
                        sp.dma_start(tile, where).then_inc(small_landed, 16)
            sp.wait_ge(fin_ready, 1)
            sp.dma_start(out, yt[:, :]).then_inc(stored, 16)
            sp.wait_ge(stored, 16)

        @block_.gpsimd
        def _(pool):
            nc.gpsimd.iota(column[:, :], [[1, P]], base=0, channel_multiplier=0,
                           allow_small_or_imprecise_dtypes=True).then_inc(const_ready, 1)
            nc.gpsimd.memset(minus_half[:, :], -0.5).then_inc(const_ready, 1)
            nc.gpsimd.memset(ones[:, :], 1.0).then_inc(const_ready, 1)
            pool.wait_ge(const_ready, 3)
            nc.gpsimd.affine_select(out=ident[:, :], in_=ones[:, :], compare_op=ALU.is_equal, fill=0.0,
                                    base=0, pattern=[[-1, P]], channel_multiplier=1).then_inc(ident_ready, 1)
            pool.wait_ge(var_ready, 1)
            nc.gpsimd.tensor_tensor(rstd[:, :], vpe[:, :], minus_half[:, :], ALU.pow).then_inc(rstd_ready, 1)
            pool.wait_ge(var_ready, 2)
            nc.gpsimd.tensor_tensor(rstd[:, :], vpe[:, :], minus_half[:, :], ALU.pow).then_inc(rstd_ready, 1)

        @block_.scalar
        def _(act):
            def split_hi(s):
                n = SPLITS_BY[s] - 1
                wait_raw(act, s)
                if n >= PARTS:
                    act.wait_ge(step_done, NTH_SPLIT[n - PARTS] + 1)
                nc.scalar.copy(w_hi[:, n % PARTS, :], raw_of(s)).then_inc(hi_done, 1)

            act.wait_ge(ident_ready, 1)
            nc.scalar.activation(expo[:, 0:1], ident[:, 0:1], ACT.Exp)
            act.wait_ge(xT_psum, 1)
            nc.scalar.copy(halves(xT[:, :, :].rearrange("p t n -> p (t n)")), blocks(wk)).then_inc(xT_f_ready, 1)
            nc.scalar.copy(halves(xT_hi[:, :, :].rearrange("p t n -> p (t n)")), blocks(wk)).then_inc(xT_hi_ready, 1)
            for s in range(LEAD_HI):
                if SPLIT[s]:
                    split_hi(s)
            act.wait_ge(small_landed, 16 * SMALLS)
            nc.scalar.copy(row_hi[:, :], row_sb[:, :]).then_inc(row_hi_ready, 1)

            def take(c):
                g = CHAINS[c][1]
                act.wait_ge(step_done, LAST[g] + 1)
                if c >= 2:
                    act.wait_ge(agg_psum, c - 1)
                nc.scalar.copy(halves(h[:, c % 2, :]), blocks(acc[g % 2])).then_inc(h_ready, 1)

            def take_turned(c):
                act.wait_ge(hT_psum, c + 1)
                if c:
                    act.wait_ge(alpha_psum, c)
                nc.scalar.copy(halves(hT[:, :, :].rearrange("p t n -> p (t n)")), blocks(wk)).then_inc(hT_ready, 1)

            def add_scores(c):
                act.wait_ge(row_psum, c + 1)
                act.wait_ge(diag_ready, c + 1)
                nc.scalar.activation(score[:, :], plane[:, 0:P], ACT.Identity, bias=alpha[:, 1:2],
                                     scale=1.0).then_inc(score_ready, 1)

            def exponent(c):
                act.wait_ge(top_ready, c + 1)
                nc.scalar.activation(expo[:, :], masked[:, :], ACT.Exp, bias=ntop[:, 0:1], scale=1.0).then_inc(expo_ready, 1)

            def take_turned_att(c):
                act.wait_ge(attT_psum, c + 1)
                if c:
                    act.wait_ge(agg_psum, c)
                nc.scalar.copy(attT[:, :], plane[:, P:2 * P]).then_inc(attT_ready, 1)

            def elu_exp(c):
                act.wait_ge(y_ready, c + 1)
                if c:
                    act.wait_ge(elu_ready, c)
                nc.scalar.activation(et[:, :], yt[:, :], ACT.Relu, scale=-1.0).then_inc(neg_ready, 1)
                act.wait_ge(neg_ready, c + 1)
                nc.scalar.activation(et[:, :], et[:, :], ACT.Exp, scale=-1.0).then_inc(elu_exp_ready, 1)

            def hidden_hi(c):
                act.wait_ge(elu_ready, c + 1)
                nc.scalar.copy(hid_hi[:, c * TB:(c + 1) * TB, :].rearrange("p t n -> p (t n)"), hf[:, :]).then_inc(hid_hi_done, 1)

            stages = {"take": take, "turned": take_turned, "add_scores": add_scores, "exponent": exponent,
                      "turned_att": take_turned_att, "elu_exp": elu_exp, "hidden_hi": hidden_hi}
            for i in range(len(STEPS)):
                for name, c in stages_at(i):
                    if name in stages:
                        stages[name](c)
                for n, g in enumerate((G_Q, G_K)):
                    if i == LAST[g] + QK_TAKE:
                        act.wait_ge(step_done, LAST[g] + 1)
                        if n:
                            act.wait_ge(qkT_psum, 1)
                        nc.scalar.copy(halves(qk[:, :]), blocks(acc[g % 2])).then_inc(qkv_ready, 1)
                    if i == LAST[g] + QK_TURNED:
                        act.wait_ge(qkT_psum, n + 1)
                        nc.scalar.copy(halves((qT, kT)[n].rearrange("p t n -> p (t n)")), blocks(wk)).then_inc(qkT_ready, 1)
                if i == LAST[G_V] + V_TAKE:
                    act.wait_ge(step_done, LAST[G_V] + 1)
                    for a in range(2):
                        last = nc.scalar.copy(v1[:, a * 6:a * 6 + 6, 0:MD],
                                              acc[G_V % 2][:, a, 0:HALF].rearrange("p (h d) -> p h d", d=MD))
                    last.then_inc(qkv_ready, 1)
                if i == AO_HI:
                    act.wait_ge(aoT_psum, 1)
                    nc.scalar.copy(halves(ao_hi[:, :]), blocks(wk)).then_inc(aoT_hi_done, 1)
                if i + LEAD_HI < len(STEPS) and SPLIT[i + LEAD_HI]:
                    split_hi(i + LEAD_HI)

            act.wait_ge(ynT_psum, 1)
            nc.scalar.copy(halves(hT[:, :, :].rearrange("p t n -> p (t n)")), blocks(wk)).then_inc(ynT_ready, 1)
            act.wait_ge(ffn1_psum, 1)
            nc.scalar.activation(f_hid[:, :], small[0:HID, 0:P], ACT.Gelu, bias=b_in_sb[:, 0:1], scale=1.0).then_inc(gelu_ready, 1)

        @block_.vector
        def _(dve):
            chain = [0]

            def link(ins):
                chain[0] += 1
                ins.then_inc(dve_chain, 1)
                dve.wait_ge(dve_chain, chain[0])

            def norm(tile, to, n, ready):
                for a in range(2):
                    last = nc.vector.bn_stats(stats[:, a, :], tile[:, a * HALF:(a + 1) * HALF])
                link(last)
                link(nc.vector.bn_aggr(mv[:, :], stats[:, :, :]))
                nc.vector.tensor_scalar(vpe[:, :], mv[:, 1:2], LN_EPS, None, ALU.add).then_inc(var_ready, 1)
                dve.wait_ge(rstd_ready, n)
                nc.vector.tensor_scalar(to, tile, mv[:, 0:1], rstd[:, 0:1], ALU.subtract, ALU.mult).then_inc(ready, 1)

            dve.wait_ge(x_landed, 16)
            norm(x_sb[:, :], xn[:, :], 1, xn_ready)
            dve.wait_ge(edges_landed, 32)
            nc.vector.tensor_copy(endf[:, :, :], ends[:, :, :]).then_inc(endf_ready, 1)
            dve.wait_ge(endf_ready, 1)
            dve.wait_ge(const_ready, 3)
            dve.wait_ge(xT_hi_ready, 1)
            nc.vector.tensor_tensor(halves(xT_lo[:, :, :].rearrange("p t n -> p (t n)")), blocks(wk),
                                    halves(xT_hi[:, :, :].rearrange("p t n -> p (t n)").bitcast(F32)),
                                    ALU.subtract).then_inc(xT_lo_ready, 1)
            for c in range(EC):
                for a in range(2):
                    last = nc.vector.tensor_scalar(hot[:, a, c, :], column[:, :], endf[:, a, c:c + 1], None, ALU.is_equal)
            last.then_inc(hot_ready, 1)

            def split_lo(s):
                n = SPLITS_BY[s] - 1
                dve.wait_ge(hi_done, n + 1)
                nc.vector.tensor_tensor(w_lo[:, n % PARTS, :], raw_of(s), w_hi[:, n % PARTS, :].bitcast(F32),
                                        ALU.subtract).then_inc(lo_done, 1)

            for s in range(LEAD_LO):
                if SPLIT[s]:
                    split_lo(s)

            def counts():
                dve.wait_ge(count_psum, 1)
                link(nc.vector.tensor_copy(count[:, :], small[:, 0:P]))
                link(nc.vector.tensor_scalar(absent[:, :], count[:, :], 1.0, 1.0, ALU.min, ALU.subtract))
                nc.vector.tensor_scalar(absent[:, :], absent[:, :], FAR, None, ALU.mult).then_inc(count_ready, 1)
                dve.wait_ge(small_landed, 16 * SMALLS)
                nc.vector.tensor_scalar(pm_sb[:, :], pm_sb[:, :], float(MF) ** -0.5, None, ALU.mult)
                dve.wait_ge(ident_ready, 1)
                for r in range(4):
                    last = nc.vector.tensor_scalar(pick[:, r, :], ones[0:5, :], ident[0:5, r:r + 1], None, ALU.mult)
                link(last)
                dve.wait_ge(row_hi_ready, 1)
                link(nc.vector.tensor_tensor(row_lo[:, :], row_sb[:, :], row_hi[:, :].bitcast(F32), ALU.subtract))
                nc.vector.tensor_scalar(pick[:, 3, :], pick[:, 3, :].bitcast(F32), ident[0:5, 4:5], None, ALU.add).then_inc(pick_ready, 1)
                dve.wait_ge(pick_ready, 1)
                dve.wait_ge(count_ready, 1)

            def scores(c):
                dve.wait_ge(alpha_psum, c + 1)
                if c:
                    dve.wait_ge(score_ready, c)
                link(nc.vector.tensor_copy(alpha[:, :], small[:, 0:2]))
                nc.vector.tensor_scalar(diag[:, :], ident[:, :], alpha[:, 0:1], None, ALU.mult).then_inc(diag_ready, 1)

            def maximum(c):
                dve.wait_ge(score_ready, c + 1)
                link(nc.vector.scalar_tensor_tensor(out=leaky[:, :], in0=score[:, :], scalar=SLOPE, in1=score[:, :],
                                                    op0=ALU.mult, op1=ALU.max))
                link(nc.vector.tensor_tensor_reduce(out=masked[:, :], in0=leaky[:, :], in1=absent[:, :], scale=1.0,
                                                    scalar=-3e38, op0=ALU.add, op1=ALU.max, accum_out=top[:, :]))
                nc.vector.tensor_scalar(ntop[:, :], top[:, :], -1.0, None, ALU.mult).then_inc(top_ready, 1)

            def normalise(c):
                dve.wait_ge(expo_ready, c + 1)
                link(nc.vector.tensor_tensor_reduce(out=weight[:, :], in0=expo[:, :], in1=count[:, :], scale=1.0,
                                                    scalar=0.0, op0=ALU.mult, op1=ALU.add, accum_out=den[:, :]))
                link(nc.vector.tensor_scalar(dene[:, :], den[:, :], DENOM_EPS, None, ALU.add))
                link(nc.vector.reciprocal(rden[:, :], dene[:, :]))
                nc.vector.tensor_scalar(att[:, :], weight[:, :], rden[:, 0:1], None, ALU.mult).then_inc(att_ready, 1)

            def add_b1(c):
                dve.wait_ge(agg_psum, c + 1)
                if c == 0:
                    dve.wait_ge(small_landed, 16 * SMALLS)
                for a in range(2):
                    last = nc.vector.tensor_tensor(
                        yt[:, a * HALF:(a + 1) * HALF].rearrange("p (t n) -> p t n", n=P),
                        wk[:, a, 0:HALF].rearrange("p (t n) -> p t n", n=P),
                        b1_sb[:, c, 3 * a:3 * a + 3].unsqueeze(2).broadcast_to([P, 3, P]), ALU.add)
                last.then_inc(y_ready, 1)

            def elu(c):
                dve.wait_ge(elu_exp_ready, c + 1)
                if c:
                    dve.wait_ge(hid_hi_done, c)
                nc.vector.scalar_tensor_tensor(out=hf[:, :], in0=et[:, :], scalar=-1.0, in1=yt[:, :],
                                               op0=ALU.add, op1=ALU.max).then_inc(elu_ready, 1)

            def hidden_lo(c):
                dve.wait_ge(hid_hi_done, c + 1)
                at = slice(c * TB, (c + 1) * TB)
                nc.vector.tensor_tensor(hid_lo[:, at, :].rearrange("p t n -> p (t n)"), hf[:, :],
                                        hid_hi[:, at, :].rearrange("p t n -> p (t n)").bitcast(F32),
                                        ALU.subtract).then_inc(hid_lo_done, 1)

            def features(t):
                dve.wait_ge(feat_psum, t + 1)
                if t:
                    dve.wait_ge(num_psum, t)
                nc.vector.tensor_scalar(feats, wk[:, :, :], FEATURE_EPS, FEATURE_EPS, ALU.add, ALU.max).then_inc(feat_ready, 1)

            def keep_kv(t):
                dve.wait_ge(kv_psum, t + 1)
                nc.vector.tensor_copy(kv[:, :, :].rearrange("p a d -> p (a d)"), small[:, 0:4 * (MD + 1)]).then_inc(kv_ready, 1)

            def divide(t):
                dve.wait_ge(num_psum, t + 1)
                both = plane[:, 0:2 * (MD + 1)].rearrange("p (h d) -> p h d", h=2)
                link(nc.vector.reciprocal(mrec[:, :], both[:, :, MD]))
                nc.vector.tensor_tensor(ao[:, t * PAIR:(t + 1) * PAIR].rearrange("p (h d) -> p h d", h=2),
                                        both[:, :, 0:MD], mrec[:, :].unsqueeze(2).broadcast_to([P, 2, MD]),
                                        ALU.mult).then_inc(ao_ready, 1)

            stages = {"scores": scores, "maximum": maximum, "normalise": normalise,
                      "add_b1": add_b1, "elu": elu, "hidden_lo": hidden_lo}
            pair_stages = {"features": features, "keep_kv": keep_kv, "divide": divide}
            for i in range(len(STEPS)):
                if i == COUNTED_AT:
                    counts()
                if i == FIRST[G_V]:
                    dve.wait_ge(count_psum, 1)
                    nc.vector.memset(v1[:, :, MD:MD + 1], 1.0)
                for name, c in stages_at(i):
                    if name in stages:
                        stages[name](c)
                for name, t in pairs_at(i):
                    if name in pair_stages:
                        pair_stages[name](t)
                if i == AO_LO:
                    dve.wait_ge(aoT_hi_done, 1)
                    nc.vector.tensor_tensor(halves(ao_lo[:, :]), blocks(wk), halves(ao_hi[:, :].bitcast(F32)),
                                            ALU.subtract).then_inc(aoT_lo_done, 1)
                if i + LEAD_LO < len(STEPS) and SPLIT[i + LEAD_LO]:
                    split_lo(i + LEAD_LO)

            dve.wait_ge(out_psum, 1)
            link(nc.vector.tensor_tensor(halves(x_sb[:, :]), blocks(acc[G_OUT % 2]), halves(x_sb[:, :]), ALU.add))
            norm(x_sb[:, :], hf[:, :], 2, yn_ready)
            dve.wait_ge(ffn2_psum, 1)
            nc.vector.tensor_tensor(halves(yt[:, :]), blocks(acc[1 - G_OUT % 2]), halves(x_sb[:, :]), ALU.add).then_inc(fin_ready, 1)

        @block_.tensor
        def _(pe):
            def turn(tile):
                for t in range(TB):
                    last = nc.tensor.transpose(block(wk, t), tile[:, t * P:(t + 1) * P], ident[:, :])
                return last

            pe.wait_ge(xn_ready, 1)
            pe.wait_ge(ident_ready, 1)
            turn(xn).then_inc(xT_psum, 1)

            def stationary(s):
                g, j = STEPS[s]
                kind = GROUPS[g][0]
                if kind == "layer2":
                    return None, hid_hi[:, j, :], hid_lo[:, j, :]
                if kind == "out":
                    cols = slice(j * P, (j + 1) * P)
                    return None, ao_hi[:, cols], ao_lo[:, cols]
                return xT[:, j, :], xT_hi[:, j, :], xT_lo[:, j, :]

            def open_group(g):
                bank = acc[g % 2]
                if 2 <= g <= HEADS + 1:
                    pe.wait_ge(h_ready, g - 1)
                if g >= G_V:
                    pe.wait_ge(qkv_ready, g - G_V + 1)
                rows_of = {G_Q: 0, G_K: 1, G_V: 2, G_OUT: 3}
                if g in rows_of:
                    pe.wait_ge(pick_ready, 1)
                    for a in range(2):
                        for part in (row_hi, row_lo):
                            nc.tensor.matmul(bank[:, a, 0:HALF], pick[:, rows_of[g], :],
                                             part[:, a * HALF:(a + 1) * HALF], start=part is row_hi, stop=False)

            def step(s):
                g, j = STEPS[s]
                bank = acc[g % 2]
                opens = j == 0 and g not in (G_Q, G_K, G_V, G_OUT)
                closes = j == GROUPS[g][2] - 1 and g != G_OUT
                if j == 0:
                    open_group(g)
                if g == 0 and j == 0:
                    pe.wait_ge(xT_f_ready, 1)
                if s == NTH_SPLIT[0]:
                    pe.wait_ge(xT_lo_ready, 1)
                if g == G_L2 and j % TB == 0:
                    pe.wait_ge(hid_lo_done, j // TB + 1)
                if g == G_OUT and j == 0:
                    pe.wait_ge(aoT_lo_done, 1)
                full, hi, lo = stationary(s)
                if SPLIT[s]:
                    n = SPLITS_BY[s] - 1
                    pe.wait_ge(lo_done, n + 1)
                    passes = [(hi, w_hi[:, n % PARTS, :]), (hi, w_lo[:, n % PARTS, :]), (lo, w_hi[:, n % PARTS, :])]
                else:
                    wait_raw(pe, s)
                    passes = [(full, raw_of(s))]
                for k, (left, right) in enumerate(passes):
                    for a in range(2):
                        last = nc.tensor.matmul(bank[:, a, 0:HALF], left, right[:, a * HALF:(a + 1) * HALF],
                                                start=opens and k == 0, stop=closes and k == len(passes) - 1)
                last.then_inc(step_done, 1)

            def count_edges():
                pe.wait_ge(hot_ready, 1)
                for c in range(EC):
                    last = nc.tensor.matmul(small[:, 0:P], hot[:, 1, c, :], hot[:, 0, c, :],
                                            start=(c == 0), stop=(c == EC - 1))
                last.then_inc(count_psum, 1)

            def turn_head(c):
                pe.wait_ge(h_ready, c + 1)
                if c == 0:
                    pe.wait_ge(xT_lo_ready, 1)
                before = c if AGG_FIRST else c - 1
                if 0 < before and c < HEADS:
                    pe.wait_ge(y_ready, before)
                if c == HEADS:
                    pe.wait_ge(aoT_lo_done, 1)
                turn(h[:, c % 2, :]).then_inc(hT_psum, 1)

            def alphas(c):
                pe.wait_ge(hT_ready, c + 1)
                if c == 0:
                    pe.wait_ge(small_landed, 16 * SMALLS)
                    pe.wait_ge(count_ready, 1)
                if c == HEADS:
                    pe.wait_ge(kv_ready, TB)
                for t in range(TB):
                    vec = a2_sb[:, t, :] if c == HEADS else a1_sb[:, c, t, :]
                    last = nc.tensor.matmul(small[:, 0:2], hT[:, t, :], vec, start=(t == 0), stop=(t == TB - 1))
                last.then_inc(alpha_psum, 1)

            def source_rows(c):
                pe.wait_ge(diag_ready, c + 1)
                if c:
                    pe.wait_ge(attT_ready, c)
                nc.tensor.matmul(plane[:, 0:P], ones[:, :], diag[:, :], start=True, stop=True).then_inc(row_psum, 1)

            def turn_att(c):
                pe.wait_ge(att_ready, c + 1)
                nc.tensor.transpose(plane[:, P:2 * P], att[:, :], ident[:, :]).then_inc(attT_psum, 1)

            def aggregate(c):
                pe.wait_ge(attT_ready, c + 1)
                pe.wait_ge(hT_ready, c + 1 if AGG_FIRST else min(c + 2, HEADS))
                if c == HEADS - 1 and Q_FIRST:
                    pe.wait_ge(qkT_ready, 1)
                for t in range(TB):
                    cols = slice(t * P, (t + 1) * P)
                    last = nc.tensor.matmul(block(wk, t), h[:, c % 2, cols], attT[:, :], start=True, stop=True)
                last.then_inc(agg_psum, 1)

            def pair_features(t):
                if t == 0:
                    pe.wait_ge(qkT_ready, 2)
                    pe.wait_ge(y_ready, HEADS)
                for h in range(2):
                    rows_ = slice(h * MD, (h + 1) * MD)
                    nc.tensor.matmul(wk[:, h, 0:MF], kT[rows_, t, :], pm_sb[rows_, :], start=True, stop=True)
                    for m in range(2):
                        last = nc.tensor.matmul(wk[:, h, MF + m * P:MF + (m + 1) * P], pm_sb[rows_, m * P:(m + 1) * P],
                                                qT[rows_, t, :], start=True, stop=True)
                last.then_inc(feat_psum, 1)

            def pair_kv(t):
                pe.wait_ge(feat_ready, t + 1)
                if t == 0:
                    pe.wait_ge(qkv_ready, 3)
                for h in range(2):
                    for m in range(2):
                        at = (2 * h + m) * (MD + 1)
                        last = nc.tensor.matmul(small[:, at:at + MD + 1], feats[:, h, m * P:(m + 1) * P],
                                                v1[:, 2 * t + h, :], start=True, stop=True)
                last.then_inc(kv_psum, 1)

            def pair_num(t):
                pe.wait_ge(kv_ready, t + 1)
                if t:
                    pe.wait_ge(ao_ready, t)
                for h in range(2):
                    for m in range(2):
                        last = nc.tensor.matmul(plane[:, h * (MD + 1):(h + 1) * (MD + 1)],
                                                feats[:, h, MF + m * P:MF + (m + 1) * P], kv[:, 2 * h + m, :],
                                                start=(m == 0), stop=(m == 1))
                last.then_inc(num_psum, 1)

            stages = {"turn": turn_head, "alphas": alphas, "row": source_rows, "turn_att": turn_att,
                      "aggregate": aggregate}
            pair_stages = {"pair_features": pair_features, "pair_kv": pair_kv, "pair_num": pair_num}
            for i in range(len(STEPS)):
                step(i)
                if i == COUNT_AT:
                    count_edges()
                for n, g in enumerate((G_Q, G_K)):
                    if i == LAST[g] + QK_TURN:
                        pe.wait_ge(qkv_ready, n + 1)
                        pe.wait_ge(y_ready, HEADS - 1 if Q_FIRST and n == 0 else HEADS)
                        turn(qk).then_inc(qkT_psum, 1)
                for name, c in stages_at(i):
                    if name in stages:
                        stages[name](c)
                for name, t in pairs_at(i):
                    if name in pair_stages:
                        pair_stages[name](t)
                if i == AO_TURN:
                    pe.wait_ge(ao_ready, TB)
                    turn(ao).then_inc(aoT_psum, 1)

            pe.wait_ge(attT_ready, HEADS + 1)
            for a in range(2):
                last = nc.tensor.matmul(acc[G_OUT % 2][:, a, 0:HALF], attT[:, :],
                                        h[:, HEADS % 2, a * HALF:(a + 1) * HALF], start=False, stop=True)
            last.then_inc(out_psum, 1)

            pe.wait_ge(yn_ready, 1)
            turn(hf).then_inc(ynT_psum, 1)
            pe.wait_ge(ynT_ready, 1)
            for t in range(TB):
                last = nc.tensor.matmul(small[0:HID, 0:P], w_in_sb[:, t, :], hT[:, t, :],
                                        start=(t == 0), stop=(t == TB - 1))
            last.then_inc(ffn1_psum, 1)
            pe.wait_ge(gelu_ready, 1)
            for a in range(2):
                last = nc.tensor.matmul(acc[1 - G_OUT % 2][:, a, 0:HALF], f_hid[:, :],
                                        w_out_sb[:, a * HALF:(a + 1) * HALF], start=True, stop=True)
            last.then_inc(ffn2_psum, 1)


def kernel(x, src, dst, L0_gnn_W1, L0_gnn_a_src1, L0_gnn_a_dst1, L0_gnn_b1, L0_gnn_W2, L0_gnn_a_src2,
           L0_gnn_a_dst2, L0_gnn_b2, L0_mix_qkv_w, L0_mix_qkv_b, L0_mix_proj_w, L0_mix_proj_b,
           L0_mix_proj_mat, L0_ffn_in_weight, L0_ffn_in_bias, L0_ffn_out_weight):
    import numpy as np
    import concourse.bacc as bacc
    from concourse.bass_utils import run_bass_kernel_spmd

    def by_partition(a):
        a = np.asarray(a)
        return np.ascontiguousarray(np.moveaxis(a.reshape(*a.shape[:-1], TB, P), -1, 0))

    qkv_b = np.asarray(L0_mix_qkv_b).reshape(3, D)
    arrays = {
        "x": np.asarray(x),
        "src": np.asarray(src).reshape(P, EC),
        "dst": np.asarray(dst).reshape(P, EC),
        "w1": np.asarray(L0_gnn_W1),
        "w2": np.asarray(L0_gnn_W2),
        "qkv": np.asarray(L0_mix_qkv_w).T,
        "proj": np.asarray(L0_mix_proj_w).T,
        "a1": np.stack([by_partition(L0_gnn_a_src1), by_partition(L0_gnn_a_dst1)], axis=-1),
        "a2": np.stack([by_partition(L0_gnn_a_src2)[:, 0], by_partition(L0_gnn_a_dst2)[:, 0]], axis=-1),
        "b1": by_partition(np.asarray(L0_gnn_b1).reshape(HEADS, D)),
        "rows": np.concatenate([qkv_b, np.asarray(L0_mix_proj_b)[None], np.asarray(L0_gnn_b2)[None]]),
        "pm": np.asarray(L0_mix_proj_mat).T,
        "w_in": np.moveaxis(by_partition(L0_ffn_in_weight), 1, 2),
        "b_in": np.asarray(L0_ffn_in_bias).reshape(HID, 1),
        "w_out": np.asarray(L0_ffn_out_weight),
    }
    arrays = {f"in_{n}_dram": np.ascontiguousarray(a) for n, a in arrays.items()}
    nc = bacc.Bacc("TRN2", target_bir_lowering=False, num_devices=1)
    args = [nc.dram_tensor(n, a.shape, mybir.dt.from_np(a.dtype), kind="ExternalInput").ap()
            for n, a in arrays.items()]
    args.append(nc.dram_tensor("out_0_dram", (P, D), F32, kind="ExternalOutput").ap())
    build_gps_layer(nc, *args)
    r = run_bass_kernel_spmd(nc, [arrays], core_ids=[0])
    return r.results[0]["out_0_dram"]
```

```python
from contextlib import ExitStack

import concourse.bass as bass
from concourse import mybir

ALU = mybir.AluOpType
ACT = mybir.ActivationFunctionType
F32 = mybir.dt.float32
F32R = mybir.dt.float32r
BF16 = mybir.dt.bfloat16
I32 = mybir.dt.int32

P = 128
D = 768
HEADS = 8
TB = D // P
HALF = D // 2
EDGES = 4096
EC = EDGES // P
MH, MD = 12, 64
MF = 256
PAIR = 2 * MD
HID = 48
LN_EPS = 1e-5
FEATURE_EPS = 1e-3
DENOM_EPS = 1e-16
SLOPE = 0.2
FAR = 1e30

STEPS_PER_LOAD = 3
QKV_AFTER = 3
GROUPS = ([("head", h, TB) for h in range(QKV_AFTER)] + [("q", 0, TB), ("k", 1, TB), ("v", 2, TB)]
          + [("head", h, TB) for h in range(QKV_AFTER, HEADS)] + [("layer2", 0, HEADS * TB), ("out", 0, TB)])
STEPS = [(g, j) for g, (_, _, n) in enumerate(GROUPS) for j in range(n)]
G_HEAD = [g for g, (kind, _, _) in enumerate(GROUPS) if kind == "head"]
G_Q, G_K, G_V = range(QKV_AFTER, QKV_AFTER + 3)
G_L2, G_OUT = HEADS + 3, HEADS + 4
FIRST = [sum(n for _, _, n in GROUPS[:g]) for g in range(len(GROUPS))]
LAST = [sum(n for _, _, n in GROUPS[:g + 1]) - 1 for g in range(len(GROUPS))]
LOADS = len(STEPS) // STEPS_PER_LOAD
RAW = 4
PARTS = 7
LEAD_HI, LEAD_LO = 6, 5

WHOLE = (0, 1, 2, 3, 4, 7, 8, 9, 10, 12, 13, 15, 18, 22, 24, 28, 30, 36, 48, 58, 64, 65)
SPLIT = [s not in WHOLE for s in range(len(STEPS))]
SPLITS_BY = [sum(SPLIT[:s + 1]) for s in range(len(STEPS))]
NTH_SPLIT = [s for s in range(len(STEPS)) if SPLIT[s]]

WARM_START, WARM_END = 13, 11

CHAINS = list(enumerate(G_HEAD + [G_L2]))
STAGES = ("take scores row add_scores maximum exponent normalise "
          "scale_att turn_att turned_att aggregate add_b1 elu_exp elu hidden_hi hidden_lo").split()
HEAD_AT = dict(zip(STAGES, (1, 2, 6, 6, 6, 7, 7, 8, 10, 9, 11, 12, 13, 14, 16, 19)))
BESIDE_AT = dict(zip(STAGES, (1, 2, 5, 4, 5, 6, 6, 7, 9, 8, 10, 10, 13, 14, 16, 19)))
TAIL_AT = dict(zip(STAGES, (0, 1, 2, 2, 3, 3, 6, 5, 6, 6)))


def stages_at(i):
    return [(name, c) for c, g in CHAINS
            for name, k in (HEAD_AT if c < QKV_AFTER else BESIDE_AT if c < HEADS else TAIL_AT).items()
            if i == LAST[g] + k]


QK_TAKE, QK_TURN, QK_TURNED, V_TAKE = 0, 2, 1, 2
PAIR_STARTS = (41, 53, 65, 71, 78, 92)
PAIR_AT = dict(zip("pair_features features pair_kv keep_kv pair_num divide".split(), (0, 0, 3, 2, 5, 5)))
AO_TURN, AO_HI, AO_LO = (PAIR_STARTS[-1] + k for k in (6, 7, 6))
HOT_SLOTS = 1
COUNT_AT, COUNTED_AT = 10, 11
SMALLS_AFTER, VECS_AFTER = 0, 4
ROW_SPLIT_AT = 1


def pairs_at(i):
    return [(name, t) for t, first in enumerate(PAIR_STARTS) for name, k in PAIR_AT.items() if i == first + k]


def build_gps_layer(nc, x, src, dst, w1, w2, qkv, proj, vectors, b1, rows, pm, w_in, b_in, w_out, out):
    ctx = ExitStack()
    with ctx:
        def sb(name, shape, dt=F32):
            return ctx.enter_context(nc.sbuf_tensor(name, shape, dt))

        def ps(name, shape):
            return ctx.enter_context(nc.psum_tensor(name, shape, F32))

        def sem(name):
            return ctx.enter_context(nc.semaphore(name))

        raw = sb("raw", [P, RAW, STEPS_PER_LOAD, D])
        w_hi = sb("w_hi", [P, PARTS, D], F32R)
        w_lo = sb("w_lo", [P, PARTS, D], F32R)
        hid_hi = sb("hid_hi", [P, HEADS * TB, P], F32R)
        hid_lo = sb("hid_lo", [P, HEADS * TB, P], F32R)
        xT = sb("xT", [P, TB, P])
        xT_hi = sb("xT_hi", [P, TB, P], F32R)
        xT_lo = sb("xT_lo", [P, TB, P], F32R)
        x_sb = sb("x_sb", [P, D])
        h = sb("h", [P, 2, D])
        ao_hi = sb("ao_hi", [P, D], F32R)
        ao_lo = sb("ao_lo", [P, D], F32R)
        vecs = sb("vecs", [P, 2, D])
        yt = sb("yt", [P, D])
        et = sb("et", [P, D])
        hf = sb("hf", [P, D])
        scratch = sb("scratch", [P, 4176])
        qk = sb("qk", [P, D])
        count = sb("count", [P, P])
        absent = sb("absent", [P, P])
        score = sb("score", [P, P])
        expo = sb("expo", [P, P])
        att = sb("att", [P, P])
        diag = sb("diag", [P, P])
        ident = sb("ident", [P, P])
        ones = sb("ones", [P, P])
        column = sb("column", [P, P], BF16)
        attT = sb("attT", [P, P])
        row_sb = sb("row_sb", [5, D])
        row_hi = sb("row_hi", [5, D], F32R)
        row_lo = sb("row_lo", [5, D], F32R)
        pick = sb("pick", [5, 4, P], F32R)
        pm_sb = sb("pm_sb", [P, MF])
        b1_sb = sb("b1_sb", [P, HEADS, TB])
        w_in_sb = sb("w_in_sb", [P, TB, HID])
        b_in_sb = sb("b_in_sb", [HID, 1])
        w_out_sb = sb("w_out_sb", [HID, D])
        f_hid = sb("f_hid", [HID, P])
        ends = sb("ends", [P, 2, EC], I32)
        endf = sb("endf", [P, 2, EC])
        kv = sb("kv", [P, 4, MD + 1])
        alpha = sb("alpha", [P, 2])
        stats = sb("stats", [P, 2, 6])
        mv = sb("mv", [P, 2])
        vpe = sb("vpe", [P, 1])
        rstd = sb("rstd", [P, 1])
        columns = sb("columns", [P, 8])
        minus_half, eps, top, ntop, den, dene, rden = (columns[:, k:k + 1] for k in range(7))
        mrec = sb("mrec", [P, 2])

        masked = weight = score
        leaky = expo

        hot = scratch[:, 0:2 * EC * P // 2].bitcast(BF16).rearrange("p (a c n) -> p a c n", a=2, c=EC)
        qT = scratch[:, 0:D].rearrange("p (t n) -> p t n", t=TB)
        kT = scratch[:, D:2 * D].rearrange("p (t n) -> p t n", t=TB)
        v1 = scratch[:, 2 * D:2 * D + MH * (MD + 1)].rearrange("p (h d) -> p h d", h=MH)
        AO0 = 2 * D + MH * (MD + 1)
        ao = scratch[:, AO0:AO0 + D]
        feats = scratch[:, AO0 + D:AO0 + D + 1024].rearrange("p (a f) -> p a f", a=2)
        xn = hf

        acc = [ps(f"acc{i}", [P, 2, 512]) for i in range(2)]
        wk = ps("wk", [P, 2, 512])
        small = ps("small", [P, 512])
        plane = ps("plane", [P, 512])

        NUM0 = 4 * (MD + 1)

        def blocks(bank):
            return bank[:, :, 0:HALF]

        def block(bank, t):
            return bank[:, t // 3, (t % 3) * P:(t % 3) * P + P]

        def halves(tile):
            return tile.rearrange("p (a c) -> p a c", a=2)

        x_landed, edges_landed, small_landed, ffn_landed = sem("x_landed"), sem("edges_landed"), sem("small_landed"), sem("ffn_landed")
        raw_landed = [sem(f"raw_landed{i}") for i in range(RAW)]
        const_ready, ident_ready, rstd_ready = sem("const_ready"), sem("ident_ready"), sem("rstd_ready")
        hot_src_ready, hot_dst_ready, endf_ready = sem("hot_src_ready"), sem("hot_dst_ready"), sem("endf_ready")
        xn_ready, var_ready, pick_ready = sem("xn_ready"), sem("var_ready"), sem("pick_ready")
        xT_psum, xT_f_ready, xT_hi_ready, xT_lo_ready = sem("xT_psum"), sem("xT_f_ready"), sem("xT_hi_ready"), sem("xT_lo_ready")
        count_psum, count_ready = sem("count_psum"), sem("count_ready")
        step_done, hi_done, lo_done = sem("step_done"), sem("hi_done"), sem("lo_done")
        h_ready = sem("h_ready")
        vecs_landed, alpha_ready = sem("vecs_landed"), sem("alpha_ready")
        diag_ready, row_psum, score_ready = sem("diag_ready"), sem("row_psum"), sem("score_ready")
        top_ready, expo_ready, att_ready = sem("top_ready"), sem("expo_ready"), sem("att_ready")
        rden_ready, relu_ready = sem("rden_ready"), sem("relu_ready")
        attT_psum, attT_ready, row_hi_ready = sem("attT_psum"), sem("attT_ready"), sem("row_hi_ready")
        agg_psum, y_ready, neg_ready, elu_exp_ready = sem("agg_psum"), sem("y_ready"), sem("neg_ready"), sem("elu_exp_ready")
        elu_ready, hid_hi_done, hid_lo_done = sem("elu_ready"), sem("hid_hi_done"), sem("hid_lo_done")
        qkv_ready, qkT_psum, qkT_ready = sem("qkv_ready"), sem("qkT_psum"), sem("qkT_ready")
        feat_psum, feat_ready, kv_psum, kv_ready = sem("feat_psum"), sem("feat_ready"), sem("kv_psum"), sem("kv_ready")
        num_psum, ao_ready, aoT_psum, aoT_hi_done, aoT_lo_done = sem("num_psum"), sem("ao_ready"), sem("aoT_psum"), sem("aoT_hi_done"), sem("aoT_lo_done")
        out_psum, res_ready, ynT_psum, ynT_ready = sem("out_psum"), sem("res_ready"), sem("ynT_psum"), sem("ynT_ready")
        yn_ready, ffn1_psum, gelu_ready, ffn2_psum, fin_ready, stored = sem("yn_ready"), sem("ffn1_psum"), sem("gelu_ready"), sem("ffn2_psum"), sem("fin_ready"), sem("stored")
        dve_chain = sem("dve_chain")

        SMALLS = 4

        def weight_view(u):
            g, j = STEPS[u * STEPS_PER_LOAD]
            kind, n, _ = GROUPS[g]
            table, col = {"head": (w1, n * D), "q": (qkv, 0), "k": (qkv, D), "v": (qkv, 2 * D),
                          "layer2": (w2, 0), "out": (proj, 0)}[kind]
            return table[j * P:(j + STEPS_PER_LOAD) * P, col:col + D].rearrange("(t p) c -> p t c", p=P)

        def raw_of(s):
            u = s // STEPS_PER_LOAD
            return raw[:, u % RAW, s % STEPS_PER_LOAD, :]

        def wait_raw(eng, s):
            u = s // STEPS_PER_LOAD
            eng.wait_ge(raw_landed[u % RAW], 16 * (u // RAW + 1))

        block_ = ctx.enter_context(nc.Block())

        @block_.sync
        def _(sp):
            sp.dma_start(x_sb[:, :], x).then_inc(x_landed, 16)
            sp.dma_start(ends[:, 0, :], src).then_inc(edges_landed, 16)
            sp.dma_start(ends[:, 1, :], dst).then_inc(edges_landed, 16)
            smalls = [(b1_sb[:, :, :], b1),
                      (row_sb[:, :], rows), (pm_sb[0:MD, :], pm), (pm_sb[MD:P, :], pm)]
            ffn_arrays = [(w_in_sb[:, :, :], w_in), (b_in_sb[:, :], b_in), (w_out_sb[:, :], w_out)]
            for u in range(LOADS):
                if u >= RAW:
                    old = [s for s in range((u - RAW) * STEPS_PER_LOAD, (u - RAW + 1) * STEPS_PER_LOAD)]
                    split = [s for s in old if SPLIT[s]]
                    whole = [s for s in old if not SPLIT[s]]
                    if split:
                        sp.wait_ge(lo_done, SPLITS_BY[split[-1]])
                    if whole:
                        sp.wait_ge(step_done, whole[-1] + 1)
                sp.dma_start(raw[:, u % RAW, :, :], weight_view(u)).then_inc(raw_landed[u % RAW], 16)
                if u == SMALLS_AFTER:
                    for tile, where in smalls:
                        sp.dma_start(tile, where).then_inc(small_landed, 16)
                for c, g in CHAINS:
                    if u == FIRST[g] // STEPS_PER_LOAD + VECS_AFTER:
                        if c:
                            sp.wait_ge(alpha_ready, c)
                        sp.dma_start(vecs[:, :, :], vectors[c:c + 1].partition_broadcast(P)
                                     ).then_inc(vecs_landed, 16)
            for tile, where in ffn_arrays:
                sp.dma_start(tile, where).then_inc(ffn_landed, 16)
            for a in range(2):
                cols = slice(a * HALF, (a + 1) * HALF)
                sp.wait_ge(fin_ready, a + 1)
                sp.dma_start(out[:, cols], yt[:, cols]).then_inc(stored, 16)
            sp.wait_ge(stored, 32)

        @block_.gpsimd
        def _(pool):
            nc.gpsimd.iota(column[:, :], [[1, P]], base=0, channel_multiplier=0,
                           allow_small_or_imprecise_dtypes=True).then_inc(const_ready, 1)
            nc.gpsimd.memset(minus_half[:, :], -0.5).then_inc(const_ready, 1)
            nc.gpsimd.memset(eps[:, :], FEATURE_EPS).then_inc(const_ready, 1)
            nc.gpsimd.memset(ones[:, :], 1.0).then_inc(const_ready, 1)
            pool.wait_ge(const_ready, 4)
            nc.gpsimd.affine_select(out=ident[:, :], in_=ones[:, :], compare_op=ALU.is_equal, fill=0.0,
                                    base=0, pattern=[[-1, P]], channel_multiplier=1).then_inc(ident_ready, 1)
            pool.wait_ge(var_ready, 1)
            nc.gpsimd.tensor_tensor(rstd[:, :], vpe[:, :], minus_half[:, :], ALU.pow).then_inc(rstd_ready, 1)
            pool.wait_ge(endf_ready, 1)
            for c in range(EC):
                last = nc.gpsimd.tensor_scalar(hot[:, 0, c, :], column[:, :], endf[:, 0, c:c + 1], None, ALU.is_equal)
            last.then_inc(hot_src_ready, 1)
            pool.wait_ge(var_ready, 2)
            nc.gpsimd.tensor_tensor(rstd[:, :], vpe[:, :], minus_half[:, :], ALU.pow).then_inc(rstd_ready, 1)

        @block_.scalar
        def _(act):
            def split_hi(s):
                n = SPLITS_BY[s] - 1
                wait_raw(act, s)
                if n >= PARTS:
                    act.wait_ge(step_done, NTH_SPLIT[n - PARTS] + 1)
                nc.scalar.copy(w_hi[:, n % PARTS, :], raw_of(s)).then_inc(hi_done, 1)

            act.wait_ge(ident_ready, 1)
            nc.scalar.activation(expo[:, 0:1], ident[:, 0:1], ACT.Exp)
            for a in range(2):
                act.wait_ge(xT_psum, a + 1)
                nc.scalar.copy(xT[:, 3 * a:3 * a + 3, :].rearrange("p t n -> p (t n)"), wk[:, a, 0:HALF]).then_inc(xT_f_ready, 1)
            nc.scalar.copy(halves(xT_hi[:, :, :].rearrange("p t n -> p (t n)")), blocks(wk)).then_inc(xT_hi_ready, 1)
            for s in range(LEAD_HI):
                if SPLIT[s]:
                    split_hi(s)

            def take(c):
                g = CHAINS[c][1]
                act.wait_ge(step_done, LAST[g] + 1)
                if c >= 2:
                    act.wait_ge(agg_psum, c - 1)
                nc.scalar.copy(halves(h[:, c % 2, :]), blocks(acc[g % 2])).then_inc(h_ready, 1)

            def add_scores(c):
                act.wait_ge(row_psum, c + 1)
                act.wait_ge(alpha_ready, c + 1)
                if c:
                    act.wait_ge(att_ready, c)
                nc.scalar.activation(score[:, :], plane[:, 0:P], ACT.Identity, bias=alpha[:, 1:2],
                                     scale=1.0).then_inc(score_ready, 1)

            def exponent(c):
                act.wait_ge(top_ready, c + 1)
                nc.scalar.activation(expo[:, :], masked[:, :], ACT.Exp, bias=ntop[:, 0:1], scale=1.0).then_inc(expo_ready, 1)

            def scale_att(c):
                act.wait_ge(rden_ready, c + 1)
                nc.scalar.activation(att[:, :], weight[:, :], ACT.Identity, scale=rden[:, 0:1]).then_inc(att_ready, 1)

            def take_turned_att(c):
                act.wait_ge(attT_psum, c + 1)
                if c:
                    act.wait_ge(agg_psum, c)
                nc.scalar.copy(attT[:, :], plane[:, P:2 * P]).then_inc(attT_ready, 1)

            def add_b1(c):
                act.wait_ge(agg_psum, c + 1)
                if c:
                    act.wait_ge(elu_ready, c)
                for t in range(TB):
                    last = nc.scalar.activation(yt[:, t * P:(t + 1) * P], block(wk, t), ACT.Identity,
                                                bias=b1_sb[:, c, t:t + 1], scale=1.0)
                last.then_inc(y_ready, 1)

            def elu_exp(c):
                act.wait_ge(y_ready, c + 1)
                if c:
                    act.wait_ge(elu_ready, c)
                nc.scalar.activation(et[:, :], yt[:, :], ACT.Relu, scale=-1.0).then_inc(neg_ready, 1)
                act.wait_ge(neg_ready, c + 1)
                nc.scalar.activation(et[:, :], et[:, :], ACT.Exp, scale=-1.0).then_inc(elu_exp_ready, 1)

            def hidden_hi(c):
                act.wait_ge(elu_ready, c + 1)
                nc.scalar.copy(hid_hi[:, c * TB:(c + 1) * TB, :].rearrange("p t n -> p (t n)"), hf[:, :]).then_inc(hid_hi_done, 1)

            def keep_kv(t):
                act.wait_ge(kv_psum, t + 1)
                nc.scalar.copy(kv[:, :, :].rearrange("p a d -> p (a d)"), small[:, 0:4 * (MD + 1)]).then_inc(kv_ready, 1)

            pair_stages = {"keep_kv": keep_kv}
            stages = {"take": take, "add_scores": add_scores, "exponent": exponent, "scale_att": scale_att, "add_b1": add_b1,
                      "turned_att": take_turned_att, "elu_exp": elu_exp, "hidden_hi": hidden_hi}
            for i in range(len(STEPS)):
                if i == ROW_SPLIT_AT:
                    act.wait_ge(small_landed, 16 * SMALLS)
                    nc.scalar.copy(row_hi[:, :], row_sb[:, :]).then_inc(row_hi_ready, 1)
                for name, c in stages_at(i):
                    if name in stages:
                        stages[name](c)
                for name, t in pairs_at(i):
                    if name in pair_stages:
                        pair_stages[name](t)
                for n, g in enumerate((G_Q, G_K)):
                    if i == LAST[g] + QK_TAKE:
                        act.wait_ge(step_done, LAST[g] + 1)
                        if n:
                            act.wait_ge(qkT_psum, 1)
                        else:
                            act.wait_ge(alpha_ready, QKV_AFTER)
                        nc.scalar.copy(halves(qk[:, :]), blocks(acc[g % 2])).then_inc(qkv_ready, 1)
                    if i == LAST[g] + QK_TURNED:
                        act.wait_ge(qkT_psum, n + 1)
                        act.wait_ge(count_psum, 1)
                        nc.scalar.copy(halves((qT, kT)[n].rearrange("p t n -> p (t n)")), blocks(wk)).then_inc(qkT_ready, 1)
                if i == LAST[G_V] + V_TAKE:
                    act.wait_ge(step_done, LAST[G_V] + 1)
                    for a in range(2):
                        last = nc.scalar.copy(v1[:, a * 6:a * 6 + 6, 0:MD],
                                              acc[G_V % 2][:, a, 0:HALF].rearrange("p (h d) -> p h d", d=MD))
                    last.then_inc(qkv_ready, 1)
                if i == AO_HI:
                    act.wait_ge(aoT_psum, 1)
                    nc.scalar.copy(halves(ao_hi[:, :]), blocks(wk)).then_inc(aoT_hi_done, 1)
                if i + LEAD_HI < len(STEPS) and SPLIT[i + LEAD_HI]:
                    split_hi(i + LEAD_HI)

            nc.scalar.activation(expo[:, 0:1], ident[:, 0:1], ACT.Gelu)
            for a in range(2):
                act.wait_ge(ynT_psum, a + 1)
                nc.scalar.copy(et[:, a * HALF:(a + 1) * HALF], wk[:, a, 0:HALF]).then_inc(ynT_ready, 1)
            act.wait_ge(ffn1_psum, 1)
            act.wait_ge(ffn_landed, 16 * 3)
            nc.scalar.activation(f_hid[:, :], small[0:HID, 0:P], ACT.Gelu, bias=b_in_sb[:, 0:1], scale=1.0).then_inc(gelu_ready, 1)

        @block_.vector
        def _(dve):
            chain = [0]

            def link(ins):
                chain[0] += 1
                ins.then_inc(dve_chain, 1)
                dve.wait_ge(dve_chain, chain[0])

            def norm(tile, to, n, ready):
                for a in range(2):
                    last = nc.vector.bn_stats(stats[:, a, :], tile[:, a * HALF:(a + 1) * HALF])
                link(last)
                link(nc.vector.bn_aggr(mv[:, :], stats[:, :, :]))
                nc.vector.tensor_scalar(vpe[:, :], mv[:, 1:2], LN_EPS, None, ALU.add).then_inc(var_ready, 1)
                dve.wait_ge(rstd_ready, n)
                for a in range(2):
                    cols = slice(a * HALF, (a + 1) * HALF)
                    nc.vector.tensor_scalar(to[:, cols], tile[:, cols], mv[:, 0:1], rstd[:, 0:1],
                                            ALU.subtract, ALU.mult).then_inc(ready, 1)

            dve.wait_ge(x_landed, 16)
            norm(x_sb, xn, 1, xn_ready)
            dve.wait_ge(edges_landed, 32)
            nc.vector.tensor_copy(endf[:, :, :], ends[:, :, :]).then_inc(endf_ready, 1)
            dve.wait_ge(endf_ready, 1)
            dve.wait_ge(const_ready, 4)
            dve.wait_ge(xT_hi_ready, 1)
            nc.vector.tensor_tensor(halves(xT_lo[:, :, :].rearrange("p t n -> p (t n)")), blocks(wk),
                                    halves(xT_hi[:, :, :].rearrange("p t n -> p (t n)").bitcast(F32)),
                                    ALU.subtract).then_inc(xT_lo_ready, 1)

            def split_lo(s):
                n = SPLITS_BY[s] - 1
                dve.wait_ge(hi_done, n + 1)
                nc.vector.tensor_tensor(w_lo[:, n % PARTS, :], raw_of(s), w_hi[:, n % PARTS, :].bitcast(F32),
                                        ALU.subtract).then_inc(lo_done, 1)

            for s in range(LEAD_LO):
                if SPLIT[s]:
                    split_lo(s)

            def hot_rows(i):
                for c in range(i * EC // HOT_SLOTS, (i + 1) * EC // HOT_SLOTS):
                    last = nc.vector.tensor_scalar(hot[:, 1, c, :], column[:, :], endf[:, 1, c:c + 1], None, ALU.is_equal)
                last.then_inc(hot_dst_ready, 1)

            def counts():
                dve.wait_ge(count_psum, 1)
                link(nc.vector.tensor_copy(count[:, :], small[:, 0:P]))
                link(nc.vector.tensor_scalar(absent[:, :], count[:, :], 1.0, 1.0, ALU.min, ALU.subtract))
                nc.vector.tensor_scalar(absent[:, :], absent[:, :], FAR, None, ALU.mult).then_inc(count_ready, 1)
                dve.wait_ge(small_landed, 16 * SMALLS)
                nc.vector.tensor_scalar(pm_sb[:, :], pm_sb[:, :], float(MF) ** -0.5, None, ALU.mult)
                dve.wait_ge(ident_ready, 1)
                for r in range(4):
                    last = nc.vector.tensor_scalar(pick[:, r, :], ones[0:5, :], ident[0:5, r:r + 1], None, ALU.mult)
                link(last)
                dve.wait_ge(row_hi_ready, 1)
                link(nc.vector.tensor_tensor(row_lo[:, :], row_sb[:, :], row_hi[:, :].bitcast(F32), ALU.subtract))
                nc.vector.tensor_scalar(pick[:, 3, :], pick[:, 3, :].bitcast(F32), ident[0:5, 4:5], None, ALU.add).then_inc(pick_ready, 1)
                dve.wait_ge(pick_ready, 1)
                dve.wait_ge(count_ready, 1)

            def scores(c):
                def dot(a):
                    return nc.vector.tensor_tensor_reduce(out=qk[:, :], in0=h[:, c % 2, :], in1=vecs[:, a, :],
                                                          scale=1.0, scalar=0.0, op0=ALU.mult, op1=ALU.add,
                                                          accum_out=alpha[:, a:a + 1])
                dve.wait_ge(h_ready, c + 1)
                dve.wait_ge(vecs_landed, 16 * (c + 1))
                if c:
                    dve.wait_ge(score_ready, c)
                    dve.wait_ge(row_psum, c)
                if c == QKV_AFTER:
                    dve.wait_ge(qkT_psum, 2)
                link(dot(0))
                nc.vector.tensor_scalar(diag[:, :], ident[:, :], alpha[:, 0:1], None, ALU.mult).then_inc(diag_ready, 1)
                dot(1).then_inc(alpha_ready, 1)

            def maximum(c):
                dve.wait_ge(score_ready, c + 1)
                link(nc.vector.scalar_tensor_tensor(out=leaky[:, :], in0=score[:, :], scalar=SLOPE, in1=score[:, :],
                                                    op0=ALU.mult, op1=ALU.max))
                link(nc.vector.tensor_tensor_reduce(out=masked[:, :], in0=leaky[:, :], in1=absent[:, :], scale=1.0,
                                                    scalar=-3e38, op0=ALU.add, op1=ALU.max, accum_out=top[:, :]))
                nc.vector.tensor_scalar(ntop[:, :], top[:, :], -1.0, None, ALU.mult).then_inc(top_ready, 1)

            def normalise(c):
                dve.wait_ge(expo_ready, c + 1)
                link(nc.vector.tensor_tensor_reduce(out=weight[:, :], in0=expo[:, :], in1=count[:, :], scale=1.0,
                                                    scalar=0.0, op0=ALU.mult, op1=ALU.add, accum_out=den[:, :]))
                link(nc.vector.tensor_scalar(dene[:, :], den[:, :], DENOM_EPS, None, ALU.add))
                nc.vector.reciprocal(rden[:, :], dene[:, :]).then_inc(rden_ready, 1)

            def elu(c):
                dve.wait_ge(elu_exp_ready, c + 1)
                if c:
                    dve.wait_ge(hid_lo_done, c)
                nc.vector.scalar_tensor_tensor(out=hf[:, :], in0=et[:, :], scalar=-1.0, in1=yt[:, :],
                                               op0=ALU.add, op1=ALU.max).then_inc(elu_ready, 1)

            def hidden_lo(c):
                dve.wait_ge(hid_hi_done, c + 1)
                at = slice(c * TB, (c + 1) * TB)
                nc.vector.tensor_tensor(hid_lo[:, at, :].rearrange("p t n -> p (t n)"), hf[:, :],
                                        hid_hi[:, at, :].rearrange("p t n -> p (t n)").bitcast(F32),
                                        ALU.subtract).then_inc(hid_lo_done, 1)

            def features(t):
                dve.wait_ge(feat_psum, t + 1)
                if t:
                    dve.wait_ge(num_psum, t)
                nc.vector.tensor_scalar(feats, wk[:, :, :], FEATURE_EPS, FEATURE_EPS, ALU.add, ALU.max).then_inc(feat_ready, 1)

            def divide(t):
                dve.wait_ge(num_psum, t + 1)
                both = small[:, NUM0:NUM0 + 2 * (MD + 1)].rearrange("p (h d) -> p h d", h=2)
                link(nc.vector.reciprocal(mrec[:, :], both[:, :, MD]))
                nc.vector.tensor_tensor(ao[:, t * PAIR:(t + 1) * PAIR].rearrange("p (h d) -> p h d", h=2),
                                        both[:, :, 0:MD], mrec[:, :].unsqueeze(2).broadcast_to([P, 2, MD]),
                                        ALU.mult).then_inc(ao_ready, 1)

            stages = {"scores": scores, "maximum": maximum, "normalise": normalise, "elu": elu, "hidden_lo": hidden_lo}
            pair_stages = {"features": features, "divide": divide}
            for i in range(len(STEPS)):
                if i < HOT_SLOTS:
                    hot_rows(i)
                if i == COUNTED_AT:
                    counts()
                if i == FIRST[G_V]:
                    dve.wait_ge(count_psum, 1)
                    nc.vector.memset(v1[:, :, MD:MD + 1], 1.0)
                for name, c in stages_at(i):
                    if name in stages:
                        stages[name](c)
                for name, t in pairs_at(i):
                    if name in pair_stages:
                        pair_stages[name](t)
                if i == AO_LO:
                    dve.wait_ge(aoT_hi_done, 1)
                    nc.vector.tensor_tensor(halves(ao_lo[:, :]), blocks(wk), halves(ao_hi[:, :].bitcast(F32)),
                                            ALU.subtract).then_inc(aoT_lo_done, 1)
                if i + LEAD_LO < len(STEPS) and SPLIT[i + LEAD_LO]:
                    split_lo(i + LEAD_LO)

            for a in range(2):
                cols = slice(a * HALF, (a + 1) * HALF)
                dve.wait_ge(out_psum, a + 1)
                link(nc.vector.tensor_tensor(x_sb[:, cols], acc[G_OUT % 2][:, a, 0:HALF], x_sb[:, cols], ALU.add))
            norm(x_sb, hf, 2, yn_ready)
            for a in range(2):
                cols = slice(a * HALF, (a + 1) * HALF)
                dve.wait_ge(ffn2_psum, a + 1)
                nc.vector.tensor_tensor(yt[:, cols], acc[1 - G_OUT % 2][:, a, 0:HALF], x_sb[:, cols],
                                        ALU.add).then_inc(fin_ready, 1)

        @block_.tensor
        def _(pe):
            def turn(tile):
                for t in range(TB):
                    last = nc.tensor.transpose(block(wk, t), tile[:, t * P:(t + 1) * P], ident[:, :])
                return last

            def turn_halves(tile, ready, done):
                for a in range(2):
                    pe.wait_ge(ready, a + 1)
                    for t in range(3 * a, 3 * a + 3):
                        last = nc.tensor.transpose(block(wk, t), tile[:, t * P:(t + 1) * P], ident[:, :])
                    last.then_inc(done, 1)

            def keep_warm(n):
                for _ in range(n):
                    nc.tensor.matmul(small[:, 0:P], ident[:, :], ones[:, :], start=True, stop=True)

            pe.wait_ge(const_ready, 4)
            pe.wait_ge(ident_ready, 1)
            keep_warm(WARM_START)
            turn_halves(xn, xn_ready, xT_psum)

            def stationary(s):
                g, j = STEPS[s]
                kind = GROUPS[g][0]
                if kind == "layer2":
                    return None, hid_hi[:, j, :], hid_lo[:, j, :]
                if kind == "out":
                    cols = slice(j * P, (j + 1) * P)
                    return None, ao_hi[:, cols], ao_lo[:, cols]
                return xT[:, j, :], xT_hi[:, j, :], xT_lo[:, j, :]

            def open_group(g):
                bank = acc[g % 2]
                if g >= 2:
                    if GROUPS[g - 2][0] == "head":
                        pe.wait_ge(h_ready, GROUPS[g - 2][1] + 1)
                    else:
                        pe.wait_ge(qkv_ready, GROUPS[g - 2][1] + 1)
                rows_of = {G_Q: 0, G_K: 1, G_V: 2, G_OUT: 3}
                if g in rows_of:
                    pe.wait_ge(pick_ready, 1)
                    for a in range(2):
                        for part in (row_hi, row_lo):
                            nc.tensor.matmul(bank[:, a, 0:HALF], pick[:, rows_of[g], :],
                                             part[:, a * HALF:(a + 1) * HALF], start=part is row_hi, stop=False)

            def step(s):
                g, j = STEPS[s]
                bank = acc[g % 2]
                opens = j == 0 and g not in (G_Q, G_K, G_V, G_OUT)
                closes = j == GROUPS[g][2] - 1 and g != G_OUT
                if j == 0:
                    open_group(g)
                if g == 0 and j % 3 == 0:
                    pe.wait_ge(xT_f_ready, 1 + j // 3)
                if s == NTH_SPLIT[0]:
                    pe.wait_ge(xT_lo_ready, 1)
                if g == G_L2 and j % TB == 0:
                    pe.wait_ge(hid_lo_done, j // TB + 1)
                if g == G_OUT and j == 0:
                    pe.wait_ge(aoT_lo_done, 1)
                full, hi, lo = stationary(s)
                if SPLIT[s]:
                    n = SPLITS_BY[s] - 1
                    pe.wait_ge(lo_done, n + 1)
                    passes = [(hi, w_hi[:, n % PARTS, :]), (hi, w_lo[:, n % PARTS, :]), (lo, w_hi[:, n % PARTS, :])]
                else:
                    wait_raw(pe, s)
                    passes = [(full, raw_of(s))]
                for k, (left, right) in enumerate(passes):
                    for a in range(2):
                        last = nc.tensor.matmul(bank[:, a, 0:HALF], left, right[:, a * HALF:(a + 1) * HALF],
                                                start=opens and k == 0, stop=closes and k == len(passes) - 1)
                last.then_inc(step_done, 1)

            def count_edges():
                pe.wait_ge(hot_src_ready, 1)
                pe.wait_ge(hot_dst_ready, HOT_SLOTS)
                for c in range(EC):
                    last = nc.tensor.matmul(small[:, 0:P], hot[:, 1, c, :], hot[:, 0, c, :],
                                            start=(c == 0), stop=(c == EC - 1))
                last.then_inc(count_psum, 1)

            wk_left = [(xT_lo_ready, 1)]

            def take_wk(sem, value):
                pe.wait_ge(*wk_left[0])
                wk_left[0] = (sem, value)

            def source_rows(c):
                pe.wait_ge(diag_ready, c + 1)
                if c:
                    pe.wait_ge(attT_ready, c)
                nc.tensor.matmul(plane[:, 0:P], ones[:, :], diag[:, :], start=True, stop=True).then_inc(row_psum, 1)

            def turn_att(c):
                pe.wait_ge(att_ready, c + 1)
                nc.tensor.transpose(plane[:, P:2 * P], att[:, :], ident[:, :]).then_inc(attT_psum, 1)

            def aggregate(c):
                pe.wait_ge(attT_ready, c + 1)
                take_wk(y_ready, c + 1)
                for t in range(TB):
                    cols = slice(t * P, (t + 1) * P)
                    last = nc.tensor.matmul(block(wk, t), h[:, c % 2, cols], attT[:, :], start=True, stop=True)
                last.then_inc(agg_psum, 1)

            def pair_features(t):
                if t == 0:
                    pe.wait_ge(qkT_ready, 2)
                take_wk(feat_ready, t + 1)
                for h in range(2):
                    rows_ = slice(h * MD, (h + 1) * MD)
                    nc.tensor.matmul(wk[:, h, 0:MF], kT[rows_, t, :], pm_sb[rows_, :], start=True, stop=True)
                    for m in range(2):
                        last = nc.tensor.matmul(wk[:, h, MF + m * P:MF + (m + 1) * P], pm_sb[rows_, m * P:(m + 1) * P],
                                                qT[rows_, t, :], start=True, stop=True)
                last.then_inc(feat_psum, 1)

            def pair_kv(t):
                pe.wait_ge(feat_ready, t + 1)
                if t == 0:
                    pe.wait_ge(count_ready, 1)
                    pe.wait_ge(qkv_ready, 3)
                else:
                    pe.wait_ge(ao_ready, t)
                for h in range(2):
                    for m in range(2):
                        at = (2 * h + m) * (MD + 1)
                        last = nc.tensor.matmul(small[:, at:at + MD + 1], feats[:, h, m * P:(m + 1) * P],
                                                v1[:, 2 * t + h, :], start=True, stop=True)
                last.then_inc(kv_psum, 1)

            def pair_num(t):
                pe.wait_ge(kv_ready, t + 1)
                for h in range(2):
                    for m in range(2):
                        last = nc.tensor.matmul(small[:, NUM0 + h * (MD + 1):NUM0 + (h + 1) * (MD + 1)],
                                                feats[:, h, MF + m * P:MF + (m + 1) * P], kv[:, 2 * h + m, :],
                                                start=(m == 0), stop=(m == 1))
                last.then_inc(num_psum, 1)

            stages = {"row": source_rows, "turn_att": turn_att,
                      "aggregate": aggregate}
            pair_stages = {"pair_features": pair_features, "pair_kv": pair_kv, "pair_num": pair_num}
            for i in range(len(STEPS)):
                step(i)
                if i == COUNT_AT:
                    count_edges()
                for n, g in enumerate((G_Q, G_K)):
                    if i == LAST[g] + QK_TURN:
                        pe.wait_ge(qkv_ready, n + 1)
                        take_wk(qkT_ready, n + 1)
                        turn(qk).then_inc(qkT_psum, 1)
                for name, c in stages_at(i):
                    if name in stages:
                        stages[name](c)
                for name, t in pairs_at(i):
                    if name in pair_stages:
                        pair_stages[name](t)
                if i == AO_TURN:
                    pe.wait_ge(ao_ready, TB)
                    take_wk(aoT_lo_done, 1)
                    turn(ao).then_inc(aoT_psum, 1)

            pe.wait_ge(attT_ready, HEADS + 1)
            for a in range(2):
                last = nc.tensor.matmul(acc[G_OUT % 2][:, a, 0:HALF], attT[:, :],
                                        h[:, HEADS % 2, a * HALF:(a + 1) * HALF], start=False, stop=True)
                last.then_inc(out_psum, 1)

            keep_warm(WARM_END)
            pe.wait_ge(ffn_landed, 16 * 3)
            take_wk(ynT_ready, 2)
            turn_halves(hf, yn_ready, ynT_psum)
            for t in range(TB):
                if t % 3 == 0:
                    pe.wait_ge(ynT_ready, 1 + t // 3)
                last = nc.tensor.matmul(small[0:HID, 0:P], w_in_sb[:, t, :], et[:, t * P:(t + 1) * P],
                                        start=(t == 0), stop=(t == TB - 1))
            last.then_inc(ffn1_psum, 1)
            pe.wait_ge(gelu_ready, 1)
            for a in range(2):
                last = nc.tensor.matmul(acc[1 - G_OUT % 2][:, a, 0:HALF], f_hid[:, :],
                                        w_out_sb[:, a * HALF:(a + 1) * HALF], start=True, stop=True)
                last.then_inc(ffn2_psum, 1)


def kernel(x, src, dst, L0_gnn_W1, L0_gnn_a_src1, L0_gnn_a_dst1, L0_gnn_b1, L0_gnn_W2, L0_gnn_a_src2,
           L0_gnn_a_dst2, L0_gnn_b2, L0_mix_qkv_w, L0_mix_qkv_b, L0_mix_proj_w, L0_mix_proj_b,
           L0_mix_proj_mat, L0_ffn_in_weight, L0_ffn_in_bias, L0_ffn_out_weight):
    import numpy as np
    import concourse.bacc as bacc
    from concourse.bass_utils import run_bass_kernel_spmd

    def by_partition(a):
        a = np.asarray(a)
        return np.ascontiguousarray(np.moveaxis(a.reshape(*a.shape[:-1], TB, P), -1, 0))

    qkv_b = np.asarray(L0_mix_qkv_b).reshape(3, D)
    arrays = {
        "x": np.asarray(x),
        "src": np.asarray(src).reshape(P, EC),
        "dst": np.asarray(dst).reshape(P, EC),
        "w1": np.asarray(L0_gnn_W1),
        "w2": np.asarray(L0_gnn_W2),
        "qkv": np.asarray(L0_mix_qkv_w).T,
        "proj": np.asarray(L0_mix_proj_w).T,
        "vectors": np.stack([np.concatenate([L0_gnn_a_src1, L0_gnn_a_src2]),
                             np.concatenate([L0_gnn_a_dst1, L0_gnn_a_dst2])], axis=1),
        "b1": by_partition(np.asarray(L0_gnn_b1).reshape(HEADS, D)),
        "rows": np.concatenate([qkv_b, np.asarray(L0_mix_proj_b)[None], np.asarray(L0_gnn_b2)[None]]),
        "pm": np.asarray(L0_mix_proj_mat).T,
        "w_in": np.moveaxis(by_partition(L0_ffn_in_weight), 1, 2),
        "b_in": np.asarray(L0_ffn_in_bias).reshape(HID, 1),
        "w_out": np.asarray(L0_ffn_out_weight),
    }
    arrays = {f"in_{n}_dram": np.ascontiguousarray(a) for n, a in arrays.items()}
    nc = bacc.Bacc("TRN2", target_bir_lowering=False, num_devices=1)
    args = [nc.dram_tensor(n, a.shape, mybir.dt.from_np(a.dtype), kind="ExternalInput").ap()
            for n, a in arrays.items()]
    args.append(nc.dram_tensor("out_0_dram", (P, D), F32, kind="ExternalOutput").ap())
    build_gps_layer(nc, *args)
    r = run_bass_kernel_spmd(nc, [arrays], core_ids=[0])
    return r.results[0]["out_0_dram"]
```
